# Optimizing a Trainium2 kernel written in Bass

```python
import numpy as np
import jax
import jax.numpy as jnp

def _softmax(x, axis=-1):
    return jax.nn.softmax(x, axis=axis)

def _gelu(x):
    return jax.nn.gelu(x, approximate=True)

def _silu(x):
    return jax.nn.silu(x)

def _sigmoid(x):
    return jax.nn.sigmoid(x)

def _layernorm(x, axis=-1, eps=1e-05):
    m = jnp.mean(x, axis=axis, keepdims=True)
    v = jnp.var(x, axis=axis, keepdims=True)
    return (x - m) / jnp.sqrt(v + eps)

def _scatter_add(tgt, idx, src, axis=0):
    return tgt.at[idx].add(src)

def _segment_sum(src, seg, n):
    return jax.ops.segment_sum(src, seg, n)
kernel_name = 'mk_prb_d2_jaxref_r8_4e878e'

def setup_inputs(seed: int=0):
    np.random.seed(seed)
    _w = jnp.asarray

    def _L0_attn_setup():
        import jax, jax.numpy as jnp
        import numpy as np
        B, T, D = (2, 256, 128)
        H = 16
        HD = D // H
        DL = 64
        NR = 64
        EPS = 1.1920929e-07

        def _rms_norm(x, w):
            ms = jnp.mean(jnp.square(x), axis=-1, keepdims=True)
            return x * jax.lax.rsqrt(ms + EPS) * w
        key = jax.random.key(seed)
        ks = jax.random.split(key, 10)
        s = 0.02
        return {'x': jax.random.normal(ks[0], (B, T, D), dtype=jnp.float32), 'W_DQ': jax.random.normal(ks[1], (DL, HD), dtype=jnp.float32) * s, 'W_UQ': jax.random.normal(ks[2], (HD, DL), dtype=jnp.float32) * s, 'W_DKV': jax.random.normal(ks[3], (2 * DL, HD), dtype=jnp.float32) * s, 'W_UKV': jax.random.normal(ks[4], (2 * HD, 2 * DL), dtype=jnp.float32) * s, 'W_QR': jax.random.normal(ks[5], (NR, HD), dtype=jnp.float32) * s, 'W_KR': jax.random.normal(ks[6], (NR, HD), dtype=jnp.float32) * s, 'W_O': jax.random.normal(ks[7], (HD, HD), dtype=jnp.float32) * s, 'q_norm_w': jnp.ones((HD,), dtype=jnp.float32), 'k_norm_w': jnp.ones((HD,), dtype=jnp.float32)}
    _L0_attn_in = _L0_attn_setup()

    def _L0_ffn_setup():
        import jax, jax.numpy as jnp
        import numpy as np
        DIM = 128

        def _reference_tuple_inner(x, W_r, W_k, W_v, mu_r, mu_k):
            B, T, C = x.shape
            x_prev = jnp.concatenate([jnp.zeros((B, 1, C), x.dtype), x[:, :-1, :]], axis=1)
            xr = mu_r * x + (1.0 - mu_r) * x_prev
            xk = mu_k * x + (1.0 - mu_k) * x_prev
            r = jax.nn.sigmoid(jnp.einsum('btc,dc->btd', xr, W_r))
            k = jnp.einsum('btc,dc->btd', xk, W_k)
            k_act = jnp.square(jax.nn.relu(k))
            out = r * jnp.einsum('btc,dc->btd', k_act, W_v)
            new_state = x[:, -1, :]
            return (out, new_state)
        key = jax.random.key(seed)
        ks = jax.random.split(key, 6)
        B, T, C = (8, 256, DIM)
        x = jax.random.normal(ks[0], (B, T, C), dtype=jnp.float32)
        s = 1.0 / np.sqrt(C)
        W_r = jax.random.uniform(ks[1], (C, C), jnp.float32, -s, s)
        W_k = jax.random.uniform(ks[2], (C, C), jnp.float32, -s, s)
        W_v = jax.random.uniform(ks[3], (C, C), jnp.float32, -s, s)
        mu_r = jax.random.uniform(ks[4], (C,), jnp.float32)
        mu_k = jax.random.uniform(ks[5], (C,), jnp.float32)
        return {'x': x, 'W_r': W_r, 'W_k': W_k, 'W_v': W_v, 'mu_r': mu_r, 'mu_k': mu_k}
    _L0_ffn_in = _L0_ffn_setup()

    def _L1_attn_setup():
        import jax, jax.numpy as jnp
        import numpy as np
        HEADS = 16
        PHI = (1.0 + np.sqrt(5.0)) / 2.0

        def phi_bias(L):
            pos = jnp.arange(L, dtype=jnp.float32) * PHI % 1.0
            dist = jnp.abs(pos[:, None] - pos[None, :])
            return jnp.log(jnp.exp(-dist) + 1e-08)
        key = jax.random.key(seed)
        k1, k2, k3, k4 = jax.random.split(key, 4)
        B, L, D = (2, 256, 128)
        x = jax.random.normal(k1, (B, L, D), dtype=jnp.float32)
        w_qkv = jax.random.normal(k2, (D, 3 * D), dtype=jnp.float32) * D ** (-0.5)
        w_proj = jax.random.normal(k3, (D, D), dtype=jnp.float32) * D ** (-0.5)
        b_proj = jax.random.normal(k4, (D,), dtype=jnp.float32) * 0.01
        return {'x': x, 'w_qkv': w_qkv, 'w_proj': w_proj, 'b_proj': b_proj}
    _L1_attn_in = _L1_attn_setup()

    def _L1_ffn_setup():
        import jax, jax.numpy as jnp
        import numpy as np
        TOP_K = 32
        TEMPERATURE = 1.0
        PARAM_SCALE = 0.02

        def _compose_weight(logits, A, B):
            vals, idx = jax.lax.top_k(logits, TOP_K)
            w = jax.nn.softmax(vals / TEMPERATURE)
            A_sel = A[idx]
            B_sel = B[idx]
            return jnp.einsum('k,kir,kro->io', w, A_sel, B_sel)
        key = jax.random.key(seed)
        ks = jax.random.split(key, 7)
        B, S, D, F, P, R = (2, 128, 128, 512, 32, 64)
        x = jax.random.normal(ks[0], (B, S, D), dtype=jnp.float32)
        fc1_A = jax.random.normal(ks[1], (P, D, R), dtype=jnp.float32) * PARAM_SCALE
        fc1_B = jax.random.normal(ks[2], (P, R, F), dtype=jnp.float32) * PARAM_SCALE
        fc2_A = jax.random.normal(ks[3], (P, F, R), dtype=jnp.float32) * PARAM_SCALE
        fc2_B = jax.random.normal(ks[4], (P, R, D), dtype=jnp.float32) * PARAM_SCALE
        fc1_logits = jax.random.normal(ks[5], (P,), dtype=jnp.float32)
        fc2_logits = jax.random.normal(ks[6], (P,), dtype=jnp.float32)
        return {'x': x, 'fc1_A': fc1_A, 'fc1_B': fc1_B, 'fc2_A': fc2_A, 'fc2_B': fc2_B, 'fc1_logits': fc1_logits, 'fc2_logits': fc2_logits}
    _L1_ffn_in = _L1_ffn_setup()
    _d = {'L0_attn_x': _L0_attn_in['x'], 'L0_attn_W_DQ': _L0_attn_in['W_DQ'], 'L0_attn_W_UQ': _L0_attn_in['W_UQ'], 'L0_attn_W_DKV': _L0_attn_in['W_DKV'], 'L0_attn_W_UKV': _L0_attn_in['W_UKV'], 'L0_attn_W_QR': _L0_attn_in['W_QR'], 'L0_attn_W_KR': _L0_attn_in['W_KR'], 'L0_attn_W_O': _L0_attn_in['W_O'], 'L0_attn_q_norm_w': _L0_attn_in['q_norm_w'], 'L0_attn_k_norm_w': _L0_attn_in['k_norm_w'], 'L0_ffn_W_r': _L0_ffn_in['W_r'], 'L0_ffn_W_k': _L0_ffn_in['W_k'], 'L0_ffn_W_v': _L0_ffn_in['W_v'], 'L0_ffn_mu_r': _L0_ffn_in['mu_r'], 'L0_ffn_mu_k': _L0_ffn_in['mu_k'], 'L1_attn_w_qkv': _L1_attn_in['w_qkv'], 'L1_attn_w_proj': _L1_attn_in['w_proj'], 'L1_attn_b_proj': _L1_attn_in['b_proj'], 'L1_ffn_fc1_A': _L1_ffn_in['fc1_A'], 'L1_ffn_fc1_B': _L1_ffn_in['fc1_B'], 'L1_ffn_fc2_A': _L1_ffn_in['fc2_A'], 'L1_ffn_fc2_B': _L1_ffn_in['fc2_B'], 'L1_ffn_fc1_logits': _L1_ffn_in['fc1_logits'], 'L1_ffn_fc2_logits': _L1_ffn_in['fc2_logits']}
    _x0 = _d['L0_attn_x']
    _d['L0_attn_x'] = jax.random.normal(jax.random.fold_in(jax.random.key(seed), 1), (16, 512, 128), dtype=_x0.dtype)
    del _x0
    return _d

def reference(L0_attn_x, L0_attn_W_DQ, L0_attn_W_UQ, L0_attn_W_DKV, L0_attn_W_UKV, L0_attn_W_QR, L0_attn_W_KR, L0_attn_W_O, L0_attn_q_norm_w, L0_attn_k_norm_w, L0_ffn_W_r, L0_ffn_W_k, L0_ffn_W_v, L0_ffn_mu_r, L0_ffn_mu_k, L1_attn_w_qkv, L1_attn_w_proj, L1_attn_b_proj, L1_ffn_fc1_A, L1_ffn_fc1_B, L1_ffn_fc2_A, L1_ffn_fc2_B, L1_ffn_fc1_logits, L1_ffn_fc2_logits):

    def _L0_attn_ref(x, W_DQ, W_UQ, W_DKV, W_UKV, W_QR, W_KR, W_O, q_norm_w, k_norm_w):
        import jax, jax.numpy as jnp
        import numpy as np
        B, T, D = (2, 256, 128)
        H = 16
        HD = D // H
        DL = 64
        NR = 64
        EPS = 1.1920929e-07

        def _rms_norm(x, w):
            ms = jnp.mean(jnp.square(x), axis=-1, keepdims=True)
            return x * jax.lax.rsqrt(ms + EPS) * w
        b, t, d = x.shape
        scale = HD ** (-0.5)
        xh = x.reshape(b, t, H, HD).transpose(0, 2, 1, 3)
        c_q = jnp.einsum('bhtd,ld->bhtl', xh, W_DQ)
        q_c = jnp.einsum('bhtl,dl->bhtd', c_q, W_UQ)
        q_c_norm = _rms_norm(q_c, q_norm_w)
        q_r = jnp.einsum('bhtd,rd->bhtr', q_c_norm, W_QR)
        q = jnp.concatenate([q_c_norm, q_r], axis=-1)
        c_kv = jnp.einsum('bhtd,ld->bhtl', xh, W_DKV)
        kv = jnp.einsum('bhtl,dl->bhtd', c_kv, W_UKV)
        k_c, v_c = (kv[..., :HD], kv[..., HD:])
        k_c_norm = _rms_norm(k_c, k_norm_w)
        k_r = jnp.einsum('bhtd,rd->bhtr', xh, W_KR)
        k = jnp.concatenate([k_c_norm, k_r], axis=-1)
        scores = jnp.einsum('bhqd,bhkd->bhqk', q, k) * scale
        causal = jnp.triu(jnp.full((t, t), -jnp.inf, dtype=scores.dtype), k=1)
        attn = jax.nn.softmax(scores + causal, axis=-1)
        ctx = jnp.einsum('bhqk,bhkd->bhqd', attn, v_c)
        out = jnp.einsum('bhtd,od->bhto', ctx, W_O)
        return out.transpose(0, 2, 1, 3).reshape(b, t, d)

    def _L0_ffn_ref(x, W_r, W_k, W_v, mu_r, mu_k):
        import jax, jax.numpy as jnp
        import numpy as np
        DIM = 128

        def _reference_tuple_inner(x, W_r, W_k, W_v, mu_r, mu_k):
            B, T, C = x.shape
            x_prev = jnp.concatenate([jnp.zeros((B, 1, C), x.dtype), x[:, :-1, :]], axis=1)
            xr = mu_r * x + (1.0 - mu_r) * x_prev
            xk = mu_k * x + (1.0 - mu_k) * x_prev
            r = jax.nn.sigmoid(jnp.einsum('btc,dc->btd', xr, W_r))
            k = jnp.einsum('btc,dc->btd', xk, W_k)
            k_act = jnp.square(jax.nn.relu(k))
            out = r * jnp.einsum('btc,dc->btd', k_act, W_v)
            new_state = x[:, -1, :]
            return (out, new_state)
        return _reference_tuple_inner(x, W_r, W_k, W_v, mu_r, mu_k)[0]

    def _L1_attn_ref(x, w_qkv, w_proj, b_proj):
        import jax, jax.numpy as jnp
        import numpy as np
        HEADS = 16
        PHI = (1.0 + np.sqrt(5.0)) / 2.0

        def phi_bias(L):
            pos = jnp.arange(L, dtype=jnp.float32) * PHI % 1.0
            dist = jnp.abs(pos[:, None] - pos[None, :])
            return jnp.log(jnp.exp(-dist) + 1e-08)
        B, L, D = x.shape
        H = HEADS
        Dh = D // H
        scale = Dh ** (-0.5)
        qkv = (x @ w_qkv).reshape(B, L, 3, H, Dh)
        q = jnp.transpose(qkv[:, :, 0], (0, 2, 1, 3))
        k = jnp.transpose(qkv[:, :, 1], (0, 2, 1, 3))
        v = jnp.transpose(qkv[:, :, 2], (0, 2, 1, 3))
        attn = jnp.einsum('bhid,bhjd->bhij', q, k) * scale
        attn = attn + phi_bias(L)[None, None]
        attn = jax.nn.softmax(attn, axis=-1)
        out = jnp.einsum('bhij,bhjd->bhid', attn, v)
        out = jnp.transpose(out, (0, 2, 1, 3)).reshape(B, L, D)
        return out @ w_proj + b_proj

    def _L1_ffn_ref(x, fc1_A, fc1_B, fc2_A, fc2_B, fc1_logits, fc2_logits):
        import jax, jax.numpy as jnp
        import numpy as np
        TOP_K = 32
        TEMPERATURE = 1.0
        PARAM_SCALE = 0.02

        def _compose_weight(logits, A, B):
            vals, idx = jax.lax.top_k(logits, TOP_K)
            w = jax.nn.softmax(vals / TEMPERATURE)
            A_sel = A[idx]
            B_sel = B[idx]
            return jnp.einsum('k,kir,kro->io', w, A_sel, B_sel)
        W1 = _compose_weight(fc1_logits, fc1_A, fc1_B)
        W2 = _compose_weight(fc2_logits, fc2_A, fc2_B)
        h = jax.nn.gelu(jnp.einsum('bsd,df->bsf', x, W1))
        return jnp.einsum('bsf,fd->bsd', h, W2)
    x = L0_attn_x
    xn = _layernorm(x, axis=-1)
    x = x + _L0_attn_ref(xn, L0_attn_W_DQ, L0_attn_W_UQ, L0_attn_W_DKV, L0_attn_W_UKV, L0_attn_W_QR, L0_attn_W_KR, L0_attn_W_O, L0_attn_q_norm_w, L0_attn_k_norm_w) + _L0_ffn_ref(xn, L0_ffn_W_r, L0_ffn_W_k, L0_ffn_W_v, L0_ffn_mu_r, L0_ffn_mu_k)
    xn = _layernorm(x, axis=-1)
    x = x + _L1_attn_ref(xn, L1_attn_w_qkv, L1_attn_w_proj, L1_attn_b_proj) + _L1_ffn_ref(xn, L1_ffn_fc1_A, L1_ffn_fc1_B, L1_ffn_fc2_A, L1_ffn_fc2_B, L1_ffn_fc1_logits, L1_ffn_fc2_logits)
    return x

_drawn_inputs = setup_inputs


def setup_inputs(seed=0):
    import zlib

    import numpy as np

    out = dict(_drawn_inputs(seed))
    spreads = {'L0_attn_q_norm_w': (1.0, 0.6), 'L0_attn_k_norm_w': (1.0, 0.6)}
    factors = {'L0_attn_W_DQ': 8.0,
     'L0_attn_W_UQ': 8.0,
     'L0_attn_W_DKV': 8.0,
     'L0_attn_W_UKV': 8.0,
     'L0_attn_W_QR': 8.0,
     'L0_attn_W_KR': 8.0,
     'L0_attn_W_O': 8.0,
     'L0_ffn_W_r': 3.145,
     'L0_ffn_mu_r': 6.176,
     'L1_attn_b_proj': 37.015,
     'L1_ffn_fc1_A': 8.0,
     'L1_ffn_fc1_B': 8.0,
     'L1_ffn_fc2_A': 8.0,
     'L1_ffn_fc2_B': 8.0,
     'L1_ffn_fc1_logits': 8.0,
     'L1_ffn_fc2_logits': 8.0,
     'L1_attn_w_qkv': 3.125,
     'L1_attn_w_proj': 3.155}
    for name, (base, spread) in spreads.items():
        noise = np.random.default_rng([zlib.crc32(name.encode()), seed]).standard_normal(out[name].shape)
        drawn = base * np.exp(spread * noise) if base else spread * noise
        out[name] = jnp.asarray(drawn.astype(out[name].dtype))
    for name, factor in factors.items():
        out[name] = (out[name] * factor).astype(out[name].dtype)
    return out
```

```python
from contextlib import ExitStack

import concourse.bass as bass
from concourse import mybir

F32 = mybir.dt.float32
BF16 = mybir.dt.bfloat16
ALU = mybir.AluOpType
ACT = mybir.ActivationFunctionType
AX_X = mybir.AxisListType.X

P = 128
NB, T, D = 16, 512, 128
H, HD = 16, 8
NT = T // P
G = 4
NG = H // G
FF = 512
NF = FF // P
PRIM, RANK = 32, 64
NC = PRIM * RANK // P
VW = 32
SCALE = float(HD) ** -0.5
LN_EPS = 1e-5
RMS_EPS = 1.1920929e-07
NEG = -1e30
GELU_C, GELU_K = 0.7978845608028654, 0.044715

Q_PARTS = (0, 0, 1, 0, 1, 2)
K_PARTS = (0, 1, 0, 2, 1, 0)
TERMS = len(Q_PARTS)
MROW = 96
KROWS = MROW + 2
FIRST, LAST = -2, NB
STEADY, PAIRS = 2, 6

USES = {
    0: [("OT0", 0, -1), ("MT0", 1, 0), ("FR", 0, 1), ("FK", 1, 1), ("OT1", 0, -1), ("MT1", 1, 0),
        ("XT", 0, 2), ("FV", 1, 1), ("PJ0", 0, 2), ("OT2", 1, 0), ("MT2", 0, 0), ("PJ1", 1, 2),
        ("PJ2", 0, 2), ("PJ3", 1, 2), ("OT3", 0, 0), ("MT3", 1, 1), ("FT", 0, 1), ("QT", 1, 2),
        ("KT", 0, 2)],
    1: [("OT0", 0, -1), ("MT0", 1, 0), ("H0", 0, 1), ("H1", 1, 1), ("OT1", 0, -1), ("MT1", 1, 0),
        ("XT", 0, 2), ("AT", 1, -1), ("PR", 0, -1), ("OT2", 1, 0), ("MT2", 0, 0), ("H2", 1, 1),
        ("H3", 0, 1), ("VP", 1, 1), ("OT3", 0, 0), ("MT3", 1, 1), ("Y", 0, 1), ("QT", 1, 2),
        ("KT", 0, 2)],
}


class Body:

    def __init__(self, layer, number, i=None):
        self.layer, self.number, self.i = layer, number, i

    def has(self, off):
        return 0 <= self.number + off < NB

    def parity(self, off):
        return (self.number + off) % 2

    def count(self, per, extra=0, off=0):
        fixed = per * (self.number + off) + extra
        return fixed if self.i is None else self.i * (2 * per) + fixed

    def use(self, name):
        table = USES[self.layer]
        bank = next(k for n, k, _ in table if n == name)
        before = sum(1 for n in range(FIRST, self.number) for _, k, off in table
                     if k == bank and 0 <= n + off < NB)
        for n, k, off in table:
            if n == name:
                break
            before += k == bank and self.has(off)
        per = sum(1 for _, k, _ in table if k == bank)
        return bank, (before if self.i is None else self.i * (2 * per) + before)


def run_bodies(eng, layer, body):
    for n in range(FIRST, STEADY):
        body(Body(layer, n))
    with eng.Fori(0, PAIRS) as i:
        for n in (STEADY, STEADY + 1):
            body(Body(layer, n, i))
    for n in range(STEADY + 2 * PAIRS, LAST + 1):
        body(Body(layer, n))


def wait(eng, sem, value):
    if not isinstance(value, int) or value > 0:
        eng.wait_ge(sem, value)


def wait_apart(eng, sem, value, passed):
    if not isinstance(value, int):
        eng.wait_ge(sem, value)
        eng.sem_inc(passed, 1)
    elif value > 0:
        eng.wait_ge(sem, value)


def build(nc, a, out):
    x_in = a["L0_attn_x"]
    x1_dram = nc.dram_tensor("x1_between_layers", (NB, T, D), F32).ap()
    parts_dram = nc.dram_tensor("parts_scratch", (2, 3, P, T), BF16).ap()
    x_src = {0: x_in, 1: x1_dram}
    x_dst = {0: x1_dram, 1: out}

    with ExitStack() as ctx:
        def sb(name, shape, dt=F32):
            return ctx.enter_context(nc.sbuf_tensor(name, shape, dt))

        def sem(name):
            return ctx.enter_context(nc.semaphore(name))

        s1 = ctx.enter_context(nc.psum_tensor("scores_for_max", [P, 2, T], F32))
        st = ctx.enter_context(nc.psum_tensor("scores_transposed", [P, 2, T], F32))
        acc = ctx.enter_context(nc.psum_tensor("pv_acc", [P, 2, T], F32))
        work = ctx.enter_context(nc.psum_tensor("work", [P, 2, T], F32))

        stacks = sb("stacks", [P, 2, 2, H * T], BF16)
        qs = [stacks[:, p, 0, :].rearrange("p (h n) -> p h n", h=H) for p in range(2)]
        ks = [stacks[:, p, 1, :].rearrange("p (h n) -> p h n", h=H) for p in range(2)]
        probs = sb("probs", [P, NT, G, T])
        vals = sb("vals", [P, 2, NT, H, VW])
        big = sb("big", [P, NT, 512])
        parts = sb("parts", [P, 2, 3, T], BF16)
        xnT = sb("xnT", [P, 2, T + 1])
        x_tile = sb("x_tile", [P, NT, D])
        xn = sb("xn", [P, NT, D])
        x_res = sb("x_res", [P, NT, D])
        x_new = sb("x_new", [P, NT, D])
        att = sb("att", [P, NT, H * HD])
        attT = sb("attT", [P, T])
        accS = sb("accS", [P, T])
        ffn = sb("ffn", [P, 2, NT, D])
        rest = sb("rest", [P, T])
        fa = sb("fa", [P, T])
        fb = sb("fb", [P, T])
        fc = sb("fc", [P, T])
        fd = sb("fd", [P, T])
        stats = sb("stats", [P, NT, 6])
        mv = sb("mv", [P, NT, 2])
        rstd = sb("rstd", [P, NT])
        sqr = sb("sqr", [P, NT, 2 * P])
        ssq = sb("ssq", [P, NT * 32])
        rrms = sb("rrms", [P, NT * 32])
        maxs = sb("maxs", [P, 2, G * NT])
        msp = sb("msp", [P, 2, G * NT], BF16)
        mT = sb("mT", [2 * G * NT, P], BF16)
        rsum = sb("rsum", [P, NT, G])
        half = sb("minus_half", [P, NT * 32])
        ident = sb("ident", [P, P])
        identb = sb("identb", [P, P], BF16)
        causal = sb("causal", [P, P])
        causalb = sb("causalb", [P, P], BF16)
        blocks = sb("blocks", [P, P])
        ebias = sb("ebias", [P, NT, T])
        wcat = sb("wcat", [P, 4, P])
        wrkv = sb("wrkv", [P, 3, P])
        mu = sb("mu", [P, 4])
        normw = sb("normw", [P, 2, HD])
        wqkv = sb("wqkv", [P, 3 * P])
        wproj = sb("wproj", [P, P])
        bproj = sb("bproj", [P, P])
        w1 = sb("w1", [P, FF])
        w2 = sb("w2", [P, NF, D])
        small = sb("small", [P, 8, HD])
        ukv_v = sb("ukv_v", [HD, P])
        rep = sb("rep", [P, 7, H, HD])
        lall = sb("lall", [P, 2, PRIM])
        lcol = sb("lcol", [P, 2, NC])
        lst = sb("lst", [P, 2, 4])

        setup_in = sem("setup_in")
        compose_in = [sem(f"compose_in{i}") for i in range(4)]
        setup_dve = sem("setup_dve")
        setup_act = sem("setup_act")
        setup_pe = sem("setup_pe")
        setup_pool = sem("setup_pool")
        rep_chain = sem("rep_chain")
        passed = sem("passed")
        ready = sem("ready")
        S = []
        for layer in range(2):
            S.append({n: sem(f"{n}_{layer}") for n in (
                "x_loaded", "res_loaded", "parts_stored", "stack_loaded", "mrow_loaded", "x_stored",
                "work_full0", "work_full1", "work_taken0", "work_taken1",
                "st_ready", "s1_ready", "pv_done",
                "exp_done", "acc_taken", "sq_done", "tanh_done", "part0_done",
                "red_done", "msplit", "ln", "xn_done", "mix_done", "vals_done", "rms", "split", "post",
                "rec", "gelu", "emul_dve",
                "pow_ln", "pow_rms", "kact_done", "masked", "emul_pool")})

        block = ctx.enter_context(nc.Block())
        ENGINES = 5
        SETUP_LOADS = 28

        def border(eng, n):
            eng.drain().then_inc(ready, 1)
            eng.wait_ge(ready, ENGINES * n)

        stage_b1 = probs[:].rearrange("p a b n -> p (a b n)")
        stage_a1 = vals[:, 0].rearrange("p a b n -> p (a b n)")
        stage_b2 = vals[:, 1].rearrange("p a b n -> p (a b n)")
        stage_a2 = stacks[:, 0].rearrange("p s n -> p (s n)").bitcast(F32)

        @block.sync
        def _(sp):
            loads = [
                (small[0:64, 0, :], a["L0_attn_W_DQ"]), (small[0:64, 1, :], a["W_UQ_T"]),
                (small[:, 2, :], a["L0_attn_W_DKV"]), (small[:, 3, :], a["W_UKV_K_T"]),
                (small[0:64, 4, :], a["L0_attn_W_KR"]), (small[0:64, 5, :], a["L0_attn_W_QR"]),
                (ukv_v[:], a["L0_attn_W_UKV"][HD:2 * HD, :]), (small[0:HD, 6, :], a["W_O_T"]),
                (ident[:], a["ident"]), (causal[:], a["causal"]), (blocks[:], a["blocks"]),
                (wrkv[:, 0, :], a["W_r_T"]), (wrkv[:, 1, :], a["W_k_T"]), (wrkv[:, 2, :], a["W_v_T"]),
                (mu[:, 0:1], a["mu_r"]), (mu[:, 1:2], a["mu_k"]),
                (normw[:, 0, :], a["L0_attn_q_norm_w"].unsqueeze(0).broadcast_to([P, HD])),
                (normw[:, 1, :], a["L0_attn_k_norm_w"].unsqueeze(0).broadcast_to([P, HD])),
                (wqkv[:], a["L1_attn_w_qkv"]), (wproj[:], a["L1_attn_w_proj"]),
                (bproj[:], a["L1_attn_b_proj"].unsqueeze(0).broadcast_to([P, D])),
                (lall[:, 0, :], a["L1_ffn_fc1_logits"].unsqueeze(0).broadcast_to([P, PRIM])),
                (lall[:, 1, :], a["L1_ffn_fc2_logits"].unsqueeze(0).broadcast_to([P, PRIM])),
                (ebias[:], a["ebias"].rearrange("(t p) n -> p t n", p=P)),
            ]
            sp.dma_start(stage_a1.rearrange("p (c n) -> p c n", c=NC),
                         a["fc1_A_T"].rearrange("(c p) n -> p c n", p=P)).then_inc(compose_in[0], 16)
            sp.dma_start(stage_b1.rearrange("p (c n) -> p c n", c=NC),
                         a["fc1_B"].rearrange("(c p) n -> p c n", p=P)).then_inc(compose_in[1], 16)
            for dst, src in loads:
                sp.dma_start(dst, src).then_inc(setup_in, 16)
            for l, name in enumerate(("L1_ffn_fc1_logits", "L1_ffn_fc2_logits")):
                pairs = a[name].rearrange("(c two) -> two c", two=2)
                for two in range(2):
                    sp.dma_start(lcol[64 * two:64 * two + 64, l, :],
                                 pairs[two:two + 1, :].broadcast_to([64, NC]),
                                 allow_slow_non_contiguous=True).then_inc(setup_in, 16)
            sp.dma_start(stage_a2.rearrange("p (c n) -> p c n", c=NC),
                         a["fc2_A_T"].rearrange("(c p) n -> p c n", p=P)).then_inc(compose_in[2], 16)
            sp.dma_start(stage_b2.rearrange("p (c n) -> p c n", c=NC),
                         a["fc2_B"].rearrange("(c p) n -> p c n", p=P)).then_inc(compose_in[3], 16)
            border(sp, 1)

            def body(B):
                s, layer = S[B.layer], B.layer

                def load_stack(side):
                    wait_apart(sp, s["parts_stored"], B.count(32, 32, 1), passed)
                    wait_apart(sp, s["st_ready"], B.count(64, 0), passed)
                    dst = (qs, ks)[side][B.parity(1)]
                    for t, part in enumerate((Q_PARTS, K_PARTS)[side]):
                        sp.dma_start(dst[8 * t:8 * t + 8, :, :],
                                     parts_dram[side, part].rearrange("(h d) n -> d h n", d=HD)
                                     ).then_inc(s["stack_loaded"], 16)

                for u in range(NG):
                    if u == 0 and B.has(2):
                        wait_apart(sp, s["xn_done"], B.count(NT, 0, 2), passed)
                        sp.dma_start(x_tile[:], x_src[layer][B.count(1, 2)].rearrange("(t p) f -> p t f", p=P)
                                     ).then_inc(s["x_loaded"], 16)
                    if u == 0 and B.has(-1):
                        wait_apart(sp, s["post"], B.count(2, 0, -1), passed)
                        sp.dma_start(x_res[:], x_src[layer][B.count(1, -1)].rearrange("(t p) f -> p t f", p=P)
                                     ).then_inc(s["res_loaded"], 16)
                    off = (u + 1) // NG
                    nu = (u + 1) % NG
                    if B.has(off):
                        bank, before = B.use(f"MT{u}")
                        wait_apart(sp, s[f"work_taken{bank}"], before + 1, passed)
                        for part in range(2):
                            sp.dma_start(
                                qs[B.parity(off)][MROW + part:MROW + part + 1, G * nu:G * nu + G, :]
                                .rearrange("p j (x n) -> p (j x) n", n=P),
                                mT[16 * part:16 * part + 16, :]).then_inc(s["mrow_loaded"], 16)
                    if u < 2 and B.has(1):
                        load_stack(u)
                    if u == 1 and B.has(-1):
                        wait_apart(sp, s["post"], B.count(2, 2, -1), passed)
                        sp.dma_start(x_dst[layer][B.count(1, -1)].rearrange("(t p) f -> p t f", p=P),
                                     x_new[:]).then_inc(s["x_stored"], 16)
                    if u == 3 and B.has(2):
                        wait_apart(sp, s["stack_loaded"], B.count(2 * TERMS * 16, 0, 2), passed)
                        for side in range(2):
                            wait_apart(sp, s["split"], B.count(4, 2 * side + 2, 2), passed)
                            sp.dma_start(parts_dram[side].rearrange("a f n -> f a n"), parts[:, side]
                                         ).then_inc(s["parts_stored"], 16)

            for layer in range(2):
                run_bodies(sp, layer, body)
                sp.wait_ge(S[layer]["x_stored"], 16 * NB)
                border(sp, 2 + layer)

        @block.tensor
        def _(pe):
            mm, tr = nc.tensor.matmul, nc.tensor.transpose
            pe.wait_ge(setup_dve, 2)
            mm(work[:, 0, 0:HD], ukv_v[:], small[0:HD, 6, :], start=True, stop=True).then_inc(setup_pe, 1)
            mm(s1[:, 0, 0:P], rep[0:64, 0].rearrange("p h d -> p (h d)"), rep[0:64, 1].rearrange("p h d -> p (h d)"),
               start=True, stop=True)
            mm(s1[:, 0, P:2 * P], rep[:, 2].rearrange("p h d -> p (h d)"), rep[:, 3].rearrange("p h d -> p (h d)"),
               start=True, stop=True)
            mm(s1[:, 0, 2 * P:3 * P], rep[0:64, 4].rearrange("p h d -> p (h d)"),
               rep[0:64, 5].rearrange("p h d -> p (h d)"), start=True, stop=True)
            pe.wait_ge(setup_dve, 3)
            mm(s1[:, 0, 3 * P:4 * P], rep[:, 2].rearrange("p h d -> p (h d)"), rep[:, 6].rearrange("p h d -> p (h d)"),
               start=True, stop=True).then_inc(setup_pe, 1)
            pe.wait_ge(setup_dve, 5)
            pe.wait_ge(compose_in[1], 16)
            for c in range(NC):
                last = mm(st[:, 0, :], stage_a1[:, P * c:P * c + P], stage_b1[:, FF * c:FF * c + FF],
                          start=(c == 0), stop=(c == NC - 1))
            last.then_inc(setup_pe, 1)
            pe.wait_ge(setup_dve, 6)
            pe.wait_ge(compose_in[2], 16)
            for f in range(NF):
                for c in range(NC):
                    last = mm(st[:, 1, P * f:P * f + P], stage_a2[:, FF * c + P * f:FF * c + P * f + P],
                              stage_b2[:, P * c:P * c + P], start=(c == 0), stop=(c == NC - 1))
            last.then_inc(setup_pe, 1)
            border(pe, 1)

            def body(B):
                s, layer = S[B.layer], B.layer

                def claim(name):
                    bank, before = B.use(name)
                    wait(pe, s[f"work_taken{bank}"], before)
                    return work[:, bank, :], s[f"work_full{bank}"]

                def taken_out(name):
                    bank, before = B.use(name)
                    pe.wait_ge(s[f"work_taken{bank}"], before + 1)

                def pv(off, pu, kt):
                    if layer == 0:
                        pe.wait_ge(s["masked"], B.count(NG * NT, pu * NT + kt + 1, off))
                    elif kt < 3:
                        pe.wait_ge(s["emul_pool"], B.count(NG * 3, pu * 3 + kt + 1, off))
                    else:
                        pe.wait_ge(s["emul_dve"], B.count(NG, pu + 1, off))
                    if kt == 0:
                        wait(pe, s["acc_taken"], B.count(NG, pu - 1, off))
                        if pu == 0 and layer == 0:
                            pe.wait_ge(s["vals_done"], B.count(1, 1, off))
                    q0 = P * kt if layer == 0 else 0
                    for j in range(G):
                        last = mm(acc[32 * j:32 * j + 32, pu % 2, q0:T], vals[:, B.parity(off), kt, G * pu + j, :],
                                  probs[:, kt, j, 0:T - q0], start=(kt == 0), stop=(kt == NT - 1),
                                  skip_group_check=True)
                    last.then_inc(s["pv_done"], 1)

                def scores_t(u, kt, j):
                    if j == 0 and kt == 0:
                        pe.wait_ge(s["mrow_loaded"], B.count(NG * 32, 32 * u + 32))
                    wait(pe, s["exp_done"], B.count(64, 16 * u + 4 * kt + j - 1))
                    q0 = P * kt if layer == 0 else 0
                    h, p = G * u + j, B.parity(0)
                    mm(st[:, j % 2, 0:T - q0], ks[p][0:KROWS, h, P * kt:P * kt + P], qs[p][0:KROWS, h, q0:T],
                       start=True, stop=True).then_inc(s["st_ready"], 1)

                def scores_max(off, su, jh, qt):
                    if su == 0 and jh == 0 and qt == 0:
                        pe.wait_ge(s["stack_loaded"], B.count(2 * TERMS * 16, 2 * TERMS * 16, off))
                    wait(pe, s["red_done"], B.count(64, 16 * su + 4 * jh + qt - 1, off))
                    h, p = G * su + jh, B.parity(off)
                    k1 = P * (qt + 1) if layer == 0 else T
                    last = mm(s1[:, qt % 2, 0:k1], qs[p][0:MROW, h, P * qt:P * qt + P], ks[p][0:MROW, h, 0:k1],
                              start=True, stop=(layer == 1))
                    if layer == 0:
                        last = mm(s1[:, qt % 2, P * qt:k1], identb[:], causalb[:], start=False, stop=True)
                    last.then_inc(s["s1_ready"], 1)

                for u in range(NG):
                    for kt in range(NT):
                        pvo, pu = (-1, NG - 1) if u == 0 else (0, u - 1)
                        if B.has(pvo):
                            pv(pvo, pu, kt)
                        at = (u, kt)
                        oo, ou = (-1, u + 2) if u < 2 else (0, u - 2)
                        if kt == 0 and B.has(oo):
                            bank, full = claim(f"OT{u}")
                            pe.wait_ge(s["acc_taken"], B.count(NG, ou + 1, oo))
                            for qt in range(NT):
                                last = tr(bank[:, P * qt:P * qt + P], accS[:, P * qt:P * qt + P], ident[:])
                            last.then_inc(full, 1)
                        mo, mu_ = (u + 1) // NG, (u + 1) % NG
                        if kt == 1 and B.has(mo):
                            bank, full = claim(f"MT{u}")
                            pe.wait_ge(s["msplit"], B.count(2 * NG, 2 * mu_ + 2, mo))
                            tr(bank[0:2 * G * NT, 0:P // 2].bitcast(BF16), msp[:].rearrange("p a b -> p (a b)"),
                               identb[:]).then_inc(full, 1)
                        if at == (1, 1) and B.has(2):
                            bank, full = claim("XT")
                            pe.wait_ge(s["xn_done"], B.count(NT, NT, 2))
                            for t in range(NT):
                                last = tr(bank[:, P * t:P * t + P], xn[:, t, :], ident[:])
                            last.then_inc(full, 1)
                        if layer == 0:
                            if at in ((0, 2), (0, 3)) and B.has(1):
                                n = kt - 2
                                bank, full = claim(("FR", "FK")[n])
                                pe.wait_ge(s["mix_done"], B.count(4, 2 * n + 2, 1))
                                mm(bank, wrkv[:, n, :], (fa, fb)[n][:], start=True, stop=True).then_inc(full, 1)
                            if at == (1, 2) and B.has(1):
                                bank, full = claim("FV")
                                pe.wait_ge(s["kact_done"], B.count(1, 1, 1))
                                mm(bank, wrkv[:, 2, :], fd[:], start=True, stop=True).then_inc(full, 1)
                            for t, where in enumerate(((1, 3), (2, 1), (2, 2), (2, 3))):
                                if at == where and B.has(2):
                                    bank, full = claim(f"PJ{t}")
                                    if t == 0:
                                        taken_out("XT")
                                    mm(bank, xnT[:, B.parity(2), 1 + P * t:1 + P * t + P],
                                       wcat[:].rearrange("p a n -> p (a n)"), start=True, stop=True).then_inc(full, 1)
                            if at == (3, 1) and B.has(1):
                                bank, full = claim("FT")
                                taken_out("FV")
                                for t in range(NT):
                                    last = tr(bank[:, P * t:P * t + P], fa[:, P * t:P * t + P], ident[:])
                                last.then_inc(full, 1)
                            if at in ((3, 2), (3, 3)) and B.has(2):
                                side = kt - 2
                                bank, full = claim(("QT", "KT")[side])
                                pe.wait_ge(s["rms"], B.count(7, 5 + 2 * side, 2))
                                for t in range(NT):
                                    last = tr(bank[:, P * t:P * t + P], big[:, t, P * side:P * side + P], ident[:])
                                last.then_inc(full, 1)
                        else:
                            for f, where in enumerate(((0, 2), (0, 3), (2, 1), (2, 2))):
                                if at == where and B.has(1):
                                    bank, full = claim(f"H{f}")
                                    mm(bank, w1[:, P * f:P * f + P], xnT[:, B.parity(1), 1:T + 1],
                                       start=True, stop=True).then_inc(full, 1)
                            if at == (1, 2) and B.has(-1):
                                bank, full = claim("AT")
                                taken_out("OT1")
                                for t in range(NT):
                                    last = tr(bank[:, P * t:P * t + P], att[:, t, :], ident[:])
                                last.then_inc(full, 1)
                            if at == (1, 3) and B.has(-1):
                                bank, full = claim("PR")
                                taken_out("AT")
                                for t in range(NT):
                                    last = mm(bank[:, P * t:P * t + P], attT[:, P * t:P * t + P], wproj[:],
                                              start=True, stop=True)
                                last.then_inc(full, 1)
                            if at == (2, 3) and B.has(1):
                                bank, full = claim("VP")
                                for t in range(NT):
                                    last = mm(bank[:, P * t:P * t + P],
                                              xnT[:, B.parity(1), 1 + P * t:1 + P * t + P], wqkv[:, 2 * P:3 * P],
                                              start=True, stop=True)
                                last.then_inc(full, 1)
                            if at == (3, 1) and B.has(1):
                                bank, full = claim("Y")
                                taken_out("H3")
                                for t in range(NT):
                                    for f in range(NF):
                                        last = mm(bank[:, P * t:P * t + P], big[:, f, P * t:P * t + P], w2[:, f, :],
                                                  start=(f == 0), stop=(f == NF - 1))
                                last.then_inc(full, 1)
                            if at in ((3, 2), (3, 3)) and B.has(2):
                                side = kt - 2
                                bank, full = claim(("QT", "KT")[side])
                                if side == 0:
                                    taken_out("XT")
                                mm(bank, wqkv[:, P * side:P * side + P], xnT[:, B.parity(2), 1:T + 1],
                                   start=True, stop=True).then_inc(full, 1)
                        so, su = (0, u + 2) if u < 2 else (1, u - 2)
                        for j in range(NT):
                            if B.has(0):
                                scores_t(u, kt, j)
                            if B.has(so):
                                scores_max(so, su, kt, j)

            for layer in range(2):
                run_bodies(pe, layer, body)
                border(pe, 2 + layer)

        @block.scalar
        def _(act):
            fn = nc.scalar.activation
            act.wait_ge(setup_dve, 4)
            for l in range(2):
                fn(lall[:, l, :], lall[:, l, :], ACT.Exp, bias=lst[:, l, 1:2], accum_out=lst[:, l, 2:3])
                fn(lcol[:, l, :], lcol[:, l, :], ACT.Exp, bias=lst[:, l, 1:2]).then_inc(setup_act, 1)
            border(act, 1)

            def body(B):
                s, layer = S[B.layer], B.layer

                def full(name):
                    bank, before = B.use(name)
                    act.wait_ge(s[f"work_full{bank}"], before + 1)
                    return work[:, bank, :], s[f"work_taken{bank}"]

                for u in range(NG):
                    for kt in range(NT):
                        at = (u, kt)
                        if at == (1, 1) and B.has(2):
                            bank, taken = full("XT")
                            fn(xnT[:, B.parity(2), 1:T + 1], bank, ACT.Copy).then_inc(taken, 1)
                        if layer == 0:
                            if at == (0, 2) and B.has(1):
                                bank, taken = full("FR")
                                fn(fc[:], bank, ACT.Tanh, scale=0.5).then_inc(taken, 1)
                            if at == (0, 3) and B.has(1):
                                bank, taken = full("FK")
                                fn(fd[:], bank, ACT.Relu).then_inc(taken, 1)
                            for t, where in enumerate(((1, 3), (2, 1), (2, 2), (2, 3))):
                                if at == where and B.has(2):
                                    bank, taken = full(f"PJ{t}")
                                    if t == 0:
                                        wait(act, s["vals_done"], B.count(1, 0, 2))
                                    fn(big[:, t, :], bank, ACT.Copy).then_inc(taken, 1)
                        else:
                            for f, where in enumerate(((0, 2), (0, 3), (2, 1), (2, 2))):
                                if at == where and B.has(1):
                                    bank, _ = full(f"H{f}")
                                    fn(fa[:], bank, ACT.Square).then_inc(s["sq_done"], 1)
                                    act.wait_ge(s["gelu"], B.count(2 * NF, 2 * f + 2, 1))
                                    fn(fc[:], fb[:], ACT.Tanh, scale=GELU_C).then_inc(s["tanh_done"], 1)
                            if at == (1, 2) and B.has(-1):
                                bank, taken = full("AT")
                                fn(attT[:], bank, ACT.Copy).then_inc(taken, 1)
                            if at == (2, 3) and B.has(1):
                                bank, taken = full("VP")
                                wait(act, s["pv_done"], B.count(NG * NT, 0))
                                fn(vals[:, B.parity(1), :, :, 0:HD].rearrange("p t h d -> p (t h) d"),
                                   bank.rearrange("p (x d) -> p x d", d=HD), ACT.Copy).then_inc(taken, 1)
                        if at in ((3, 2), (3, 3)) and B.has(2):
                            side = kt - 2
                            bank, _ = full(("QT", "KT")[side])
                            wait(act, s["parts_stored"], B.count(32, 0, 2))
                            fn(parts[:, side, 0, :], bank, ACT.Copy).then_inc(s["part0_done"], 1)
                        if B.has(0):
                            q0 = P * kt if layer == 0 else 0
                            for j in range(G):
                                if j == 0:
                                    wait(act, s["pv_done"], B.count(NG * NT, NT * (u - 1) + kt + 1))
                                act.wait_ge(s["st_ready"], B.count(64, 16 * u + 4 * kt + j + 1))
                                fn(probs[:, kt, j, 0:T - q0], st[:, j % 2, 0:T - q0], ACT.Exp,
                                   scale=SCALE).then_inc(s["exp_done"], 1)
                        eo, eu = (-1, NG - 1) if u == 0 else (0, u - 1)
                        if kt == NT - 1 and B.has(eo):
                            act.wait_ge(s["pv_done"], B.count(NG * NT, NT * eu + NT, eo))
                            if B.has(-1 if u < 2 else 0):
                                full(f"OT{u}")
                            fn(accS[:], acc[:, eu % 2, :], ACT.Copy).then_inc(s["acc_taken"], 1)

            for layer in range(2):
                run_bodies(act, layer, body)
                border(act, 2 + layer)

        @block.vector
        def _(dve):
            v = nc.vector
            dve.wait_ge(setup_in, 16 * SETUP_LOADS)
            v.tensor_copy(causalb[:], causal[:])
            v.tensor_copy(identb[:], ident[:]).then_inc(setup_dve, 1)
            for n in range(6):
                rows = P if n in (2, 3) else 64
                last = v.tensor_copy(rep[0:rows, n], small[0:rows, n, :].unsqueeze(1).broadcast_to([rows, H, HD]))
            last.then_inc(setup_dve, 1)
            dve.wait_ge(setup_pe, 1)
            v.tensor_copy(rep[:, 6], work[:, 0, 0:HD].unsqueeze(1).broadcast_to([P, H, HD])).then_inc(setup_dve, 1)
            for l in range(2):
                last = v.reduce_max(lst[:, l, 0:1], lall[:, l, :], AX_X)
            last.then_inc(rep_chain, 1)
            dve.wait_ge(rep_chain, 1)
            for l in range(2):
                last = v.tensor_scalar(lst[:, l, 1:2], lst[:, l, 0:1], -1.0, None, ALU.mult)
            last.then_inc(setup_dve, 1)
            dve.wait_ge(setup_act, 2)
            for l in range(2):
                last = v.reciprocal(lst[:, l, 3:4], lst[:, l, 2:3])
            last.then_inc(rep_chain, 1)
            dve.wait_ge(rep_chain, 2)
            for l in range(2):
                last = v.tensor_scalar(lcol[:, l, :], lcol[:, l, :], lst[:, l, 3:4], None, ALU.mult)
            last.then_inc(rep_chain, 1)
            dve.wait_ge(rep_chain, 3)
            for l, stage in ((0, stage_a1), (1, stage_b2)):
                dve.wait_ge(compose_in[3 * l], 16)
                rows = stage.rearrange("p (c n) -> p c n", c=NC)
                v.tensor_tensor(rows, rows, lcol[:, l, :].unsqueeze(2).broadcast_to([P, NC, P]),
                                ALU.mult).then_inc(setup_dve, 1)
            dve.wait_ge(setup_pe, 2)
            v.tensor_tensor(wcat[:], s1[:, 0, :].rearrange("p (a n) -> p a n", a=4),
                            blocks[:].unsqueeze(1).broadcast_to([P, 4, P]), ALU.mult)
            v.tensor_scalar(mu[:, 2:4], mu[:, 0:2], -1.0, 1.0, ALU.mult, ALU.add)
            v.memset(xnT[:, :, 0:1], 0.0)
            dve.wait_ge(setup_pe, 3)
            v.tensor_copy(w1[:], st[:, 0, :])
            dve.wait_ge(setup_pe, 4)
            v.tensor_scalar(w2[:].rearrange("p f d -> p (f d)"), st[:, 1, :], 0.5, None, ALU.mult)
            v.memset(stacks[:, 0].rearrange("p s n -> p (s n)").bitcast(mybir.dt.uint32), 0)
            v.memset(vals[:], 0.0).then_inc(rep_chain, 1)
            dve.wait_ge(rep_chain, 4)
            v.memset(stacks[MROW:KROWS, 0, 1, :], 1.0)
            v.memset(vals[:, :, :, :, HD:HD + 1].rearrange("p a t h d -> p (a t h) d"), 1.0)
            border(dve, 1)

            def body(B):
                s, layer = S[B.layer], B.layer

                def full(name):
                    bank, before = B.use(name)
                    dve.wait_ge(s[f"work_full{bank}"], before + 1)
                    return work[:, bank, :], s[f"work_taken{bank}"]

                def taken_out(name):
                    bank, before = B.use(name)
                    dve.wait_ge(s[f"work_taken{bank}"], before + 1)

                def link(op, name, per, n, off):
                    op.then_inc(s[name], 1)
                    dve.wait_ge(s[name], B.count(per, n, off))

                for u in range(NG):
                    for kt in range(NT):
                        at = (u, kt)
                        mo, mu_ = (u + 1) // NG, (u + 1) % NG
                        if kt == 0 and B.has(mo):
                            m = maxs[:, mu_ % 2, :]
                            dve.wait_ge(s["red_done"], B.count(64, 16 * mu_ + 16, mo))
                            link(v.tensor_scalar(msp[:, 0, :], m, -1.0, None, ALU.mult),
                                 "msplit", 2 * NG, 2 * mu_ + 1, mo)
                            v.scalar_tensor_tensor(out=msp[:, 1, :], in0=m, scalar=-1.0, in1=msp[:, 0, :],
                                                   op0=ALU.mult, op1=ALU.subtract).then_inc(s["msplit"], 1)
                        oo, ou = (-1, u + 2) if u < 2 else (0, u - 2)
                        if kt == 0 and B.has(oo):
                            bank, taken = full(f"OT{u}")
                            heads = bank.rearrange("p (t j c) -> p t j c", t=NT, j=G)
                            link(v.reciprocal(rsum[:], heads[:, :, :, HD]), "rec", NG, ou + 1, oo)
                            v.tensor_tensor(
                                att[:, :, G * HD * ou:G * HD * (ou + 1)].rearrange("p t (j d) -> p t j d", j=G),
                                heads[:, :, :, 0:HD], rsum[:].unsqueeze(3).broadcast_to([P, NT, G, HD]),
                                ALU.mult).then_inc(taken, 1)
                        if kt == 1 and B.has(mo):
                            bank, taken = full(f"MT{u}")
                            wait(dve, s["mrow_loaded"], B.count(NG * 32, 32 * mu_, mo))
                            v.tensor_copy(mT[:], bank[0:2 * G * NT, 0:P // 2].bitcast(BF16)).then_inc(taken, 1)
                        if at == (0, 2) and B.has(2):
                            dve.wait_ge(s["x_loaded"], B.count(16, 16, 2))
                            for t in range(NT):
                                last = v.bn_stats(stats[:, t, :], x_tile[:, t, :])
                            last.then_inc(s["ln"], 1)
                            wait_apart(dve, s["ln"], B.count(3, 1, 2), passed)
                            for t in range(NT):
                                last = v.bn_aggr(mv[:, t, :], stats[:, t, :])
                            link(last, "ln", 3, 2, 2)
                            v.tensor_scalar(mv[:, :, 1], mv[:, :, 1], LN_EPS, None, ALU.add).then_inc(s["ln"], 1)
                        if at == (1, 0) and B.has(2):
                            dve.wait_ge(s["pow_ln"], B.count(1, 1, 2))
                            for t in range(NT):
                                v.tensor_scalar(xn[:, t, :], x_tile[:, t, :], mv[:, t, 0:1], rstd[:, t:t + 1],
                                                ALU.subtract, ALU.mult).then_inc(s["xn_done"], 1)
                        if at in ((3, 2), (3, 3)) and B.has(2):
                            side = kt - 2
                            bank, taken = full(("QT", "KT")[side])
                            dve.wait_ge(s["part0_done"], B.count(2, side + 1, 2))
                            wait(dve, s["split"], B.count(4, 2 * side, 2))
                            v.tensor_tensor(rest[:], bank, parts[:, side, 0, :], ALU.subtract).then_inc(taken, 1)
                            taken_out(("QT", "KT")[side])
                            link(v.tensor_copy(parts[:, side, 1, :], rest[:]), "split", 4, 2 * side + 1, 2)
                            v.tensor_tensor(parts[:, side, 2, :], rest[:], parts[:, side, 1, :],
                                            ALU.subtract).then_inc(s["split"], 1)
                        if layer == 0:
                            if at == (0, 1) and B.has(1):
                                xt = xnT[:, B.parity(1), :]
                                for n, mix in enumerate((fa, fb)):
                                    link(v.tensor_scalar(mix[:], xt[:, 1:T + 1], mu[:, n:n + 1], None, ALU.mult),
                                         "mix_done", 4, 2 * n + 1, 1)
                                    v.scalar_tensor_tensor(out=mix[:], in0=xt[:, 0:T], scalar=mu[:, 2 + n:3 + n],
                                                           in1=mix[:], op0=ALU.mult, op1=ALU.add
                                                           ).then_inc(s["mix_done"], 1)
                            if at == (1, 0) and B.has(1):
                                wait(dve, s["pv_done"], B.count(NG * NT, 0))
                                v.tensor_copy(vals[:, B.parity(1), :, :, 0:HD],
                                              big[:, :, 3 * P:4 * P].rearrange("p t (h d) -> p t h d", h=H)
                                              ).then_inc(s["vals_done"], 1)
                            if at == (1, 1) and B.has(-1):
                                dve.wait_ge(s["res_loaded"], B.count(16, 16, -1))
                                wait(dve, s["x_stored"], B.count(16, 0, -1))
                                taken_out("OT1")
                                link(v.tensor_tensor(x_new[:], x_res[:], att[:], ALU.add), "post", 2, 1, -1)
                                v.tensor_tensor(x_new[:], x_new[:], ffn[:, B.parity(-1)], ALU.add
                                                ).then_inc(s["post"], 1)
                            if at == (1, 2) and B.has(1):
                                bank, taken = full("FV")
                                v.scalar_tensor_tensor(out=fa[:], in0=fc[:], scalar=1.0, in1=bank,
                                                       op0=ALU.add, op1=ALU.mult).then_inc(taken, 1)
                            if at == (3, 0) and B.has(2):
                                taken_out("PJ3")
                                qk = big[:, :, 0:2 * P]
                                link(v.tensor_tensor(sqr[:], qk, qk, ALU.mult), "rms", 7, 1, 2)
                                link(v.reduce_sum(ssq[:].rearrange("p (t x) -> p t x", t=NT),
                                                  sqr[:].rearrange("p t (x d) -> p t x d", d=HD), AX_X),
                                     "rms", 7, 2, 2)
                                v.tensor_scalar(ssq[:], ssq[:], 1.0 / HD, RMS_EPS, ALU.mult, ALU.add
                                                ).then_inc(s["rms"], 1)
                            if at == (3, 1) and B.has(2):
                                dve.wait_ge(s["pow_rms"], B.count(1, 1, 2))
                                qk = big[:, :, 0:2 * P].rearrange("p t (x d) -> p t x d", d=HD)
                                link(v.tensor_tensor(qk, qk, rrms[:].rearrange("p (t x) -> p t x", t=NT)
                                                     .unsqueeze(3).broadcast_to([P, NT, 2 * H, HD]), ALU.mult),
                                     "rms", 7, 4, 2)
                                for n in range(2):
                                    part = big[:, :, P * n:P * n + P].rearrange("p t (h d) -> p t h d", h=H)
                                    link(v.tensor_tensor(part, part, normw[:, n, :].unsqueeze(1).unsqueeze(1)
                                                         .broadcast_to([P, NT, H, HD]), ALU.mult),
                                         "rms", 7, 5 + n, 2)
                                v.tensor_tensor(big[:, :, P:2 * P], big[:, :, P:2 * P], big[:, :, 2 * P:3 * P],
                                                ALU.add).then_inc(s["rms"], 1)
                            if at == (3, 1) and B.has(1):
                                bank, taken = full("FT")
                                v.tensor_scalar(ffn[:, B.parity(1)].rearrange("p t d -> p (t d)"), bank, 0.5, None,
                                                ALU.mult).then_inc(taken, 1)
                        else:
                            for f, where in enumerate(((0, 2), (0, 3), (2, 1), (2, 2))):
                                if at == where and B.has(1):
                                    bank, taken = full(f"H{f}")
                                    dve.wait_ge(s["sq_done"], B.count(NF, f + 1, 1))
                                    link(v.tensor_scalar(fb[:], fa[:], GELU_K, 1.0, ALU.mult, ALU.add),
                                         "gelu", 2 * NF, 2 * f + 1, 1)
                                    v.tensor_tensor(fb[:], fb[:], bank, ALU.mult).then_inc(s["gelu"], 1)
                                    dve.wait_ge(s["tanh_done"], B.count(NF, f + 1, 1))
                                    v.scalar_tensor_tensor(out=big[:, f, :], in0=fc[:], scalar=1.0, in1=bank,
                                                           op0=ALU.add, op1=ALU.mult).then_inc(taken, 1)
                            if at == (1, 3) and B.has(-1):
                                bank, taken = full("PR")
                                dve.wait_ge(s["res_loaded"], B.count(16, 16, -1))
                                wait(dve, s["x_stored"], B.count(16, 0, -1))
                                v.tensor_tensor(x_new[:].rearrange("p t d -> p (t d)"), bank,
                                                x_res[:].rearrange("p t d -> p (t d)"), ALU.add).then_inc(taken, 1)
                                taken_out("PR")
                                link(v.tensor_tensor(x_new[:], x_new[:], ffn[:, B.parity(-1)], ALU.add),
                                     "post", 2, 1, -1)
                                v.tensor_tensor(x_new[:], x_new[:], bproj[:].unsqueeze(1).broadcast_to([P, NT, D]),
                                                ALU.add).then_inc(s["post"], 1)
                            if at == (3, 1) and B.has(1):
                                bank, taken = full("Y")
                                v.tensor_copy(ffn[:, B.parity(1)].rearrange("p t d -> p (t d)"), bank
                                              ).then_inc(taken, 1)
                        so, su = (0, u + 2) if u < 2 else (1, u - 2)
                        for j in range(NT):
                            if B.has(so):
                                dve.wait_ge(s["s1_ready"], B.count(64, 16 * su + 4 * kt + j + 1, so))
                                k1 = P * (j + 1) if layer == 0 else T
                                v.reduce_max(maxs[:, su % 2, NT * kt + j:NT * kt + j + 1], s1[:, j % 2, 0:k1], AX_X
                                             ).then_inc(s["red_done"], 1)
                            pvo, pu = (-1, NG - 1) if u == 0 else (0, u - 1)
                            if layer == 1 and kt == 1 and B.has(pvo):
                                dve.wait_ge(s["exp_done"], B.count(64, 16 * pu + 16, pvo))
                                last = v.tensor_tensor(probs[:, 3, j, :], probs[:, 3, j, :], ebias[:, 3, :], ALU.mult)
                                if j == G - 1:
                                    last.then_inc(s["emul_dve"], 1)

            for layer in range(2):
                run_bodies(dve, layer, body)
                border(dve, 2 + layer)

        @block.gpsimd
        def _(pool):
            g = nc.gpsimd
            g.memset(half[:], -0.5)
            g.memset(stacks[:, 1].rearrange("p s n -> p (s n)"), 0.0).then_inc(setup_pool, 1)
            pool.wait_ge(setup_pool, 1)
            g.memset(stacks[MROW:KROWS, 1, 1, :], 1.0)
            border(pool, 1)

            def body(B):
                s, layer = S[B.layer], B.layer
                for u in range(NG):
                    for kt in range(NT):
                        at = (u, kt)
                        if at == (0, 2) and B.has(2):
                            pool.wait_ge(s["ln"], B.count(3, 3, 2))
                            g.tensor_tensor(rstd[:], mv[:, :, 1], half[:, 0:NT], ALU.pow).then_inc(s["pow_ln"], 1)
                        if layer == 0 and at == (0, 3) and B.has(1):
                            bank, before = B.use("FK")
                            pool.wait_ge(s[f"work_taken{bank}"], before + 1)
                            g.tensor_tensor(fd[:], fd[:], fd[:], ALU.mult).then_inc(s["kact_done"], 1)
                        if layer == 0 and at == (3, 0) and B.has(2):
                            pool.wait_ge(s["rms"], B.count(7, 3, 2))
                            g.tensor_tensor(rrms[:], ssq[:], half[:], ALU.pow).then_inc(s["pow_rms"], 1)
                        if B.has(0) and layer == 0:
                            wait_apart(pool, s["exp_done"], B.count(64, 16 * u + 4 * kt + 4), passed)
                            diag = probs[:, kt, :, 0:P]
                            g.affine_select(out=diag, in_=diag, compare_op=ALU.is_ge, fill=0.0, base=0,
                                            pattern=[[0, G], [1, P]], channel_multiplier=-1
                                            ).then_inc(s["masked"], 1)
                        if B.has(0) and layer == 1 and kt < 3:
                            pool.wait_ge(s["exp_done"], B.count(64, 16 * u + 4 * kt + 4))
                            g.tensor_tensor(probs[:, kt], probs[:, kt],
                                            ebias[:, kt, :].unsqueeze(1).broadcast_to([P, G, T]), ALU.mult
                                            ).then_inc(s["emul_pool"], 1)

            for layer in range(2):
                run_bodies(pool, layer, body)
                border(pool, 2 + layer)


def kernel(**inputs):
    import numpy as _np
    import concourse.bacc as _bacc
    from concourse import mybir as _mybir
    from concourse.bass_utils import run_bass_kernel_spmd as _run

    f = {k: _np.asarray(v) for k, v in inputs.items()}
    send = {k: f[k] for k in ("L0_attn_x", "L0_attn_W_DQ", "L0_attn_W_DKV", "L0_attn_W_UKV", "L0_attn_W_QR",
                              "L0_attn_W_KR", "L0_attn_q_norm_w", "L0_attn_k_norm_w", "L1_attn_w_qkv",
                              "L1_attn_w_proj", "L1_attn_b_proj", "L1_ffn_fc1_logits", "L1_ffn_fc2_logits")}
    send["W_UQ_T"] = f["L0_attn_W_UQ"].T
    send["W_UKV_K_T"] = f["L0_attn_W_UKV"][:HD].T
    send["W_O_T"] = f["L0_attn_W_O"].T
    send["W_r_T"] = f["L0_ffn_W_r"].T
    send["W_k_T"] = f["L0_ffn_W_k"].T
    send["W_v_T"] = f["L0_ffn_W_v"].T
    send["mu_r"] = f["L0_ffn_mu_r"].reshape(P, 1)
    send["mu_k"] = f["L0_ffn_mu_k"].reshape(P, 1)
    send["fc1_A_T"] = f["L1_ffn_fc1_A"].transpose(0, 2, 1).reshape(NC * P, D)
    send["fc1_B"] = f["L1_ffn_fc1_B"].reshape(NC * P, FF)
    send["fc2_A_T"] = f["L1_ffn_fc2_A"].transpose(0, 2, 1).reshape(NC * P, FF)
    send["fc2_B"] = f["L1_ffn_fc2_B"].reshape(NC * P, D)
    n = _np.arange(P)
    send["ident"] = _np.eye(P, dtype=_np.float32)
    send["causal"] = _np.where(n[None, :] > n[:, None], NEG, 0.0).astype(_np.float32)
    send["blocks"] = (n[None, :] // HD == n[:, None] // HD).astype(_np.float32)
    pos = _np.mod(_np.arange(T, dtype=_np.float32) * _np.float32((1.0 + _np.sqrt(5.0)) / 2.0), _np.float32(1.0))
    send["ebias"] = (_np.exp(-_np.abs(pos[:, None] - pos[None, :])) + _np.float32(1e-8)).astype(_np.float32)

    nc = _bacc.Bacc("TRN2", target_bir_lowering=False, num_devices=1)
    arrays, args = {}, {}
    for name, value in send.items():
        value = _np.ascontiguousarray(value)
        arrays[f"in_{name}_dram"] = value
        args[name] = nc.dram_tensor(f"in_{name}_dram", value.shape, _mybir.dt.from_np(value.dtype),
                                    kind="ExternalInput").ap()
    out = nc.dram_tensor("out_0_dram", (NB, T, D), _mybir.dt.float32, kind="ExternalOutput").ap()
    build(nc, args, out)
    r = _run(nc, [arrays], core_ids=[0])
    return r.results[0]["out_0_dram"]
```

```python
from contextlib import ExitStack

import concourse.bass as bass
from concourse import mybir

F32 = mybir.dt.float32
BF16 = mybir.dt.bfloat16
ALU = mybir.AluOpType
ACT = mybir.ActivationFunctionType
AX_X = mybir.AxisListType.X

P = 128
NB, T, D = 16, 512, 128
H, HD = 16, 8
NT = T // P
G = 4
NG = H // G
FF = 512
NF = FF // P
PRIM, RANK = 32, 64
NC = PRIM * RANK // P
VW = 32
SCALE = float(HD) ** -0.5
LN_EPS = 1e-5
RMS_EPS = 1.1920929e-07
NEG = -1e30
GELU_C, GELU_K = 0.7978845608028654, 0.044715

Q_PARTS = (0, 0, 1, 0, 1, 2)
K_PARTS = (0, 1, 0, 2, 1, 0)
TERMS = len(Q_PARTS)
POOL_HEADS = 2
MROW = 96
KROWS = MROW + 2
FIRST, LAST = -2, NB
STEADY, PAIRS = 2, 6

USES = {
    0: [("OT0", -1), ("MT0", 0), ("FR", 1), ("FK", 1), ("XT", 2), ("OT1", -1), ("FV", 1), ("MT1", 0),
        ("PJ0", 2), ("PJ1", 2), ("PJ2", 2), ("OT2", 0), ("PJ3", 2), ("MT2", 0), ("FT", 1), ("OT3", 0),
        ("MT3", 1), ("QT", 2), ("KT", 2)],
    1: [("OT0", -1), ("MT0", 0), ("H0", 1), ("H1", 1), ("XT", 2), ("OT1", -1), ("H2", 1), ("MT1", 0),
        ("AT", -1), ("H3", 1), ("PR", -1), ("OT2", 0), ("VP", 1), ("MT2", 0), ("Y", 1), ("QT", 2),
        ("KT", 2), ("OT3", 0), ("MT3", 1)],
}
PJ_AT = ((1, 1), (1, 2), (1, 3), (2, 0))
H_AT = ((0, 1), (0, 2), (1, 0), (1, 2))
Q_AT, K_AT = {0: (3, 2), 1: (2, 2)}, {0: (3, 3), 1: (2, 3)}


class Body:

    def __init__(self, layer, number, i=None):
        self.layer, self.number, self.i = layer, number, i

    def has(self, off):
        return 0 <= self.number + off < NB

    def parity(self, off):
        return (self.number + off) % 2

    def count(self, per, extra=0, off=0):
        fixed = per * (self.number + off) + extra
        return fixed if self.i is None else self.i * (2 * per) + fixed

    def use(self, name):
        table = USES[self.layer]
        before = sum(1 for n in range(FIRST, self.number) for _, off in table if 0 <= n + off < NB)
        for n, off in table:
            if n == name:
                break
            before += self.has(off)
        return before if self.i is None else self.i * (2 * len(table)) + before


def run_bodies(eng, layer, body):
    for n in range(FIRST, STEADY):
        body(Body(layer, n))
    with eng.Fori(0, PAIRS) as i:
        for n in (STEADY, STEADY + 1):
            body(Body(layer, n, i))
    for n in range(STEADY + 2 * PAIRS, LAST + 1):
        body(Body(layer, n))


def wait(eng, sem, value):
    if not isinstance(value, int) or value > 0:
        eng.wait_ge(sem, value)


def wait_apart(eng, sem, value, passed):
    if not isinstance(value, int):
        eng.wait_ge(sem, value)
        eng.sem_inc(passed, 1)
    elif value > 0:
        eng.wait_ge(sem, value)


def build(nc, a, out):
    x_in = a["L0_attn_x"]
    x1_dram = nc.dram_tensor("x1_between_layers", (NB, T, D), F32).ap()
    parts_dram = nc.dram_tensor("parts_scratch", (2, 3, P, T), BF16).ap()
    x_src = {0: x_in, 1: x1_dram}
    x_dst = {0: x1_dram, 1: out}

    with ExitStack() as ctx:
        def sb(name, shape, dt=F32):
            return ctx.enter_context(nc.sbuf_tensor(name, shape, dt))

        def sem(name):
            return ctx.enter_context(nc.semaphore(name))

        s1 = ctx.enter_context(nc.psum_tensor("scores_for_max", [P, NT, T], F32))
        st = ctx.enter_context(nc.psum_tensor("scores_transposed", [P, 2, T], F32))
        acc = ctx.enter_context(nc.psum_tensor("pv_acc", [P, T], F32))
        work = ctx.enter_context(nc.psum_tensor("work", [P, T], F32))

        stacks = sb("stacks", [P, 2, 2, H * T], BF16)
        qs = [stacks[:, p, 0, :].rearrange("p (h n) -> p h n", h=H) for p in range(2)]
        ks = [stacks[:, p, 1, :].rearrange("p (h n) -> p h n", h=H) for p in range(2)]
        probs = sb("probs", [P, NT, G, T])
        vals = sb("vals", [P, 2, NT, H, VW])
        big = sb("big", [P, NT, 512])
        parts = sb("parts", [P, 2, 3, T], BF16)
        xnT = sb("xnT", [P, 2, T + 1])
        x_tile = sb("x_tile", [P, NT, D])
        xn = sb("xn", [P, NT, D])
        x_res = sb("x_res", [P, NT, D])
        x_new = sb("x_new", [P, NT, D])
        att = sb("att", [P, NT, H * HD])
        attT = sb("attT", [P, T])
        accS = sb("accS", [P, T])
        ffn = sb("ffn", [P, 2, NT, D])
        rest = sb("rest", [P, 2, T])
        fa = sb("fa", [P, T])
        fb = sb("fb", [P, T])
        fc = sb("fc", [P, T])
        fd = sb("fd", [P, T])
        stats = sb("stats", [P, NT, 6])
        mv = sb("mv", [P, NT, 2])
        rstd = sb("rstd", [P, NT])
        sqr = sb("sqr", [P, NT, 2 * P])
        ssq = sb("ssq", [P, NT * 32])
        rrms = sb("rrms", [P, NT * 32])
        maxs = sb("maxs", [P, 2, G * NT])
        msp = sb("msp", [P, 2, G * NT], BF16)
        mT = sb("mT", [2 * G * NT, P], BF16)
        rsum = sb("rsum", [P, NT, G])
        half = sb("minus_half", [P, NT * 32])
        ident = sb("ident", [P, P])
        identb = sb("identb", [P, P], BF16)
        causal = sb("causal", [P, P])
        causalb = sb("causalb", [P, P], BF16)
        blocks = sb("blocks", [P, P])
        ebias = sb("ebias", [P, NT, T])
        wcat = sb("wcat", [P, 4, P])
        wrkv = sb("wrkv", [P, 3, P])
        mu = sb("mu", [P, 4])
        normw = sb("normw", [P, 2, HD])
        wqkv = sb("wqkv", [P, 3 * P])
        wproj = sb("wproj", [P, P])
        bproj = sb("bproj", [P, P])
        w1 = sb("w1", [P, FF])
        w2 = sb("w2", [P, NF, D])
        small = sb("small", [P, 8, HD])
        ukv_v = sb("ukv_v", [HD, P])
        rep = sb("rep", [P, 7, H, HD])
        lall = sb("lall", [P, 2, PRIM])
        lcol = sb("lcol", [P, 2, NC])
        lst = sb("lst", [P, 2, 4])

        setup_in = sem("setup_in")
        compose_in = [sem(f"compose_in{i}") for i in range(4)]
        setup_dve = sem("setup_dve")
        setup_act = sem("setup_act")
        setup_pe = sem("setup_pe")
        setup_pool = sem("setup_pool")
        rep_chain = sem("rep_chain")
        passed = sem("passed")
        ready = sem("ready")
        S = []
        for layer in range(2):
            S.append({n: sem(f"{n}_{layer}") for n in (
                "x_loaded", "res_loaded", "parts_stored", "stack_loaded", "mrow_loaded", "x_stored",
                "work_full", "work_taken",
                "st_ready", "s1_ready", "pv_done",
                "exp_done", "acc_taken", "sq_done", "tanh_done", "part0_done", "part1_done", "root_done",
                "vals_done",
                "red_done", "msplit", "ln", "xn_done", "mix_done", "rms", "rest_done",
                "rec", "gelu", "emul_dve",
                "part2_done", "post",
                "pow_ln", "kact_done", "masked", "emul_pool", "k_done")})

        block = ctx.enter_context(nc.Block())
        ENGINES = 5
        SETUP_LOADS = 28

        def border(eng, n):
            eng.drain().then_inc(ready, 1)
            eng.wait_ge(ready, ENGINES * n)

        stage_b1 = probs[:].rearrange("p a b n -> p (a b n)")
        stage_a1 = vals[:, 0].rearrange("p a b n -> p (a b n)")
        stage_b2 = vals[:, 1].rearrange("p a b n -> p (a b n)")
        stage_a2 = stacks[:, 0].rearrange("p s n -> p (s n)").bitcast(F32)

        @block.sync
        def _(sp):
            loads = [
                (small[0:64, 0, :], a["L0_attn_W_DQ"]), (small[0:64, 1, :], a["W_UQ_T"]),
                (small[:, 2, :], a["L0_attn_W_DKV"]), (small[:, 3, :], a["W_UKV_K_T"]),
                (small[0:64, 4, :], a["L0_attn_W_KR"]), (small[0:64, 5, :], a["L0_attn_W_QR"]),
                (ukv_v[:], a["L0_attn_W_UKV"][HD:2 * HD, :]), (small[0:HD, 6, :], a["W_O_T"]),
                (ident[:], a["ident"]), (causal[:], a["causal"]), (blocks[:], a["blocks"]),
                (wrkv[:, 0, :], a["W_r_T"]), (wrkv[:, 1, :], a["W_k_T"]), (wrkv[:, 2, :], a["W_v_T"]),
                (mu[:, 0:1], a["mu_r"]), (mu[:, 1:2], a["mu_k"]),
                (normw[:, 0, :], a["L0_attn_q_norm_w"].unsqueeze(0).broadcast_to([P, HD])),
                (normw[:, 1, :], a["L0_attn_k_norm_w"].unsqueeze(0).broadcast_to([P, HD])),
                (wqkv[:], a["L1_attn_w_qkv"]), (wproj[:], a["L1_attn_w_proj"]),
                (bproj[:], a["L1_attn_b_proj"].unsqueeze(0).broadcast_to([P, D])),
                (lall[:, 0, :], a["L1_ffn_fc1_logits"].unsqueeze(0).broadcast_to([P, PRIM])),
                (lall[:, 1, :], a["L1_ffn_fc2_logits"].unsqueeze(0).broadcast_to([P, PRIM])),
                (ebias[:], a["ebias"].rearrange("(t p) n -> p t n", p=P)),
            ]
            sp.dma_start(stage_a1.rearrange("p (c n) -> p c n", c=NC),
                         a["fc1_A_T"].rearrange("(c p) n -> p c n", p=P)).then_inc(compose_in[0], 16)
            sp.dma_start(stage_b1.rearrange("p (c n) -> p c n", c=NC),
                         a["fc1_B"].rearrange("(c p) n -> p c n", p=P)).then_inc(compose_in[1], 16)
            for dst, src in loads:
                sp.dma_start(dst, src).then_inc(setup_in, 16)
            for l, name in enumerate(("L1_ffn_fc1_logits", "L1_ffn_fc2_logits")):
                pairs = a[name].rearrange("(c two) -> two c", two=2)
                for two in range(2):
                    sp.dma_start(lcol[64 * two:64 * two + 64, l, :],
                                 pairs[two:two + 1, :].broadcast_to([64, NC]),
                                 allow_slow_non_contiguous=True).then_inc(setup_in, 16)
            sp.dma_start(stage_a2.rearrange("p (c n) -> p c n", c=NC),
                         a["fc2_A_T"].rearrange("(c p) n -> p c n", p=P)).then_inc(compose_in[2], 16)
            sp.dma_start(stage_b2.rearrange("p (c n) -> p c n", c=NC),
                         a["fc2_B"].rearrange("(c p) n -> p c n", p=P)).then_inc(compose_in[3], 16)
            border(sp, 1)

            def body(B):
                s, layer = S[B.layer], B.layer

                def load_stack(side):
                    wait_apart(sp, s["parts_stored"], B.count(32, 32, 1), passed)
                    wait_apart(sp, s["st_ready"], B.count(64, 0), passed)
                    dst = (qs, ks)[side][B.parity(1)]
                    for t, part in enumerate((Q_PARTS, K_PARTS)[side]):
                        sp.dma_start(dst[8 * t:8 * t + 8, :, :],
                                     parts_dram[side, part].rearrange("(h d) n -> d h n", d=HD)
                                     ).then_inc(s["stack_loaded"], 16)

                for u in range(NG):
                    if u == 0 and B.has(2):
                        wait_apart(sp, s["xn_done"], B.count(NT, 0, 2), passed)
                        sp.dma_start(x_tile[:], x_src[layer][B.count(1, 2)].rearrange("(t p) f -> p t f", p=P)
                                     ).then_inc(s["x_loaded"], 16)
                    if u == 0 and B.has(-1):
                        wait_apart(sp, s["post"], B.count(2, 0, -1), passed)
                        sp.dma_start(x_res[:], x_src[layer][B.count(1, -1)].rearrange("(t p) f -> p t f", p=P)
                                     ).then_inc(s["res_loaded"], 16)
                    off = (u + 1) // NG
                    nu = (u + 1) % NG
                    if B.has(off):
                        wait_apart(sp, s["work_taken"], B.use(f"MT{u}") + 1, passed)
                        for part in range(2):
                            sp.dma_start(
                                qs[B.parity(off)][MROW + part:MROW + part + 1, G * nu:G * nu + G, :]
                                .rearrange("p j (x n) -> p (j x) n", n=P),
                                mT[16 * part:16 * part + 16, :]).then_inc(s["mrow_loaded"], 16)
                    if u == 0 and B.has(1):
                        load_stack(0)
                        load_stack(1)
                    if u == 1 and B.has(-1):
                        wait_apart(sp, s["post"], B.count(2, 2, -1), passed)
                        sp.dma_start(x_dst[layer][B.count(1, -1)].rearrange("(t p) f -> p t f", p=P),
                                     x_new[:]).then_inc(s["x_stored"], 16)
                    if u == 3 and B.has(2):
                        wait_apart(sp, s["stack_loaded"], B.count(2 * TERMS * 16, 0, 2), passed)
                        for side in range(2):
                            wait_apart(sp, s["part2_done"], B.count(2, side + 1, 2), passed)
                            sp.dma_start(parts_dram[side].rearrange("a f n -> f a n"), parts[:, side]
                                         ).then_inc(s["parts_stored"], 16)

            for layer in range(2):
                run_bodies(sp, layer, body)
                sp.wait_ge(S[layer]["x_stored"], 16 * NB)
                border(sp, 2 + layer)

        @block.tensor
        def _(pe):
            mm, tr = nc.tensor.matmul, nc.tensor.transpose
            pe.wait_ge(setup_dve, 2)
            mm(work[:, 0:HD], ukv_v[:], small[0:HD, 6, :], start=True, stop=True).then_inc(setup_pe, 1)
            mm(s1[:, 0, 0:P], rep[0:64, 0].rearrange("p h d -> p (h d)"), rep[0:64, 1].rearrange("p h d -> p (h d)"),
               start=True, stop=True)
            mm(s1[:, 0, P:2 * P], rep[:, 2].rearrange("p h d -> p (h d)"), rep[:, 3].rearrange("p h d -> p (h d)"),
               start=True, stop=True)
            mm(s1[:, 0, 2 * P:3 * P], rep[0:64, 4].rearrange("p h d -> p (h d)"),
               rep[0:64, 5].rearrange("p h d -> p (h d)"), start=True, stop=True)
            pe.wait_ge(setup_dve, 3)
            mm(s1[:, 0, 3 * P:4 * P], rep[:, 2].rearrange("p h d -> p (h d)"), rep[:, 6].rearrange("p h d -> p (h d)"),
               start=True, stop=True).then_inc(setup_pe, 1)
            pe.wait_ge(setup_dve, 5)
            pe.wait_ge(compose_in[1], 16)
            for c in range(NC):
                last = mm(st[:, 0, :], stage_a1[:, P * c:P * c + P], stage_b1[:, FF * c:FF * c + FF],
                          start=(c == 0), stop=(c == NC - 1))
            last.then_inc(setup_pe, 1)
            pe.wait_ge(setup_dve, 6)
            pe.wait_ge(compose_in[2], 16)
            for f in range(NF):
                for c in range(NC):
                    last = mm(st[:, 1, P * f:P * f + P], stage_a2[:, FF * c + P * f:FF * c + P * f + P],
                              stage_b2[:, P * c:P * c + P], start=(c == 0), stop=(c == NC - 1))
            last.then_inc(setup_pe, 1)
            border(pe, 1)

            def body(B):
                s, layer = S[B.layer], B.layer

                def claim(name):
                    wait(pe, s["work_taken"], B.use(name))

                def taken_out(name):
                    pe.wait_ge(s["work_taken"], B.use(name) + 1)

                def pv(off, pu, kt):
                    if layer == 0:
                        pe.wait_ge(s["masked"], B.count(NG * NT, pu * NT + kt + 1, off))
                    else:
                        pe.wait_ge(s["emul_pool"], B.count(NG * NT, pu * NT + kt + 1, off))
                        if kt == NT - 1:
                            pe.wait_ge(s["emul_dve"], B.count(NG, pu + 1, off))
                    if kt == 0:
                        wait(pe, s["acc_taken"], B.count(NG, pu, off))
                        if pu == 0 and layer == 0:
                            pe.wait_ge(s["vals_done"], B.count(1, 1, off))
                    q0 = P * kt if layer == 0 else 0
                    for j in range(G):
                        last = mm(acc[32 * j:32 * j + 32, q0:T], vals[:, B.parity(off), kt, G * pu + j, :],
                                  probs[:, kt, j, 0:T - q0], start=(kt == 0), stop=(kt == NT - 1),
                                  skip_group_check=True)
                    last.then_inc(s["pv_done"], 1)

                def scores_t(u, kt, j):
                    if j == 0 and kt == 0:
                        pe.wait_ge(s["mrow_loaded"], B.count(NG * 32, 32 * u + 32))
                    wait(pe, s["exp_done"], B.count(64, 16 * u + 4 * kt + j - 1))
                    q0 = P * kt if layer == 0 else 0
                    h, p = G * u + j, B.parity(0)
                    mm(st[:, j % 2, 0:T - q0], ks[p][0:KROWS, h, P * kt:P * kt + P], qs[p][0:KROWS, h, q0:T],
                       start=True, stop=True).then_inc(s["st_ready"], 1)

                def scores_max(off, su, jh, qt):
                    if su == 0 and jh == 0 and qt == 0:
                        pe.wait_ge(s["stack_loaded"], B.count(2 * TERMS * 16, 2 * TERMS * 16, off))
                    wait(pe, s["red_done"], B.count(64, 16 * su + 4 * jh + qt - 3, off))
                    h, p = G * su + jh, B.parity(off)
                    k1 = P * (qt + 1) if layer == 0 else T
                    last = mm(s1[:, qt, 0:k1], qs[p][0:MROW, h, P * qt:P * qt + P], ks[p][0:MROW, h, 0:k1],
                              start=True, stop=(layer == 1))
                    if layer == 0:
                        last = mm(s1[:, qt, P * qt:k1], identb[:], causalb[:], start=False, stop=True)
                    last.then_inc(s["s1_ready"], 1)

                def early(u, kt):
                    at, full = (u, kt), s["work_full"]
                    oo, ou = (-1, u + 2) if u < 2 else (0, u - 2)
                    if kt == 0 and B.has(oo):
                        claim(f"OT{u}")
                        pe.wait_ge(s["acc_taken"], B.count(NG, ou + 1, oo))
                        for qt in range(NT):
                            last = tr(work[:, P * qt:P * qt + P], accS[:, P * qt:P * qt + P], ident[:])
                        last.then_inc(full, 1)
                    mo, mu_ = (u + 1) // NG, (u + 1) % NG
                    if kt == 1 and B.has(mo):
                        claim(f"MT{u}")
                        pe.wait_ge(s["msplit"], B.count(2 * NG, 2 * mu_ + 2, mo))
                        tr(work[0:2 * G * NT, 0:P // 2].bitcast(BF16), msp[:].rearrange("p a b -> p (a b)"),
                           identb[:]).then_inc(full, 1)
                    if at == (0, 3) and B.has(2):
                        claim("XT")
                        pe.wait_ge(s["xn_done"], B.count(NT, NT, 2))
                        for t in range(NT):
                            last = tr(work[:, P * t:P * t + P], xn[:, t, :], ident[:])
                        last.then_inc(full, 1)
                    if layer == 0:
                        if at == (0, 2) and B.has(1):
                            channel_mix("FK", 1)
                        if at in PJ_AT[1:3] and B.has(2):
                            project(PJ_AT.index(at))
                        if at == (2, 2) and B.has(1):
                            claim("FT")
                            taken_out("FV")
                            for t in range(NT):
                                last = tr(work[:, P * t:P * t + P], fa[:, P * t:P * t + P], ident[:])
                            last.then_inc(full, 1)
                        if at == Q_AT[0] and B.has(2):
                            claim("QT")
                            pe.wait_ge(s["rms"], B.count(4, 4, 2))
                            for t in range(NT):
                                last = tr(work[:, P * t:P * t + P], big[:, t, 0:P], ident[:])
                            last.then_inc(full, 1)
                        if at == K_AT[0] and B.has(2):
                            claim("KT")
                            pe.wait_ge(s["k_done"], B.count(2, 2, 2))
                            for t in range(NT):
                                last = tr(work[:, P * t:P * t + P], big[:, t, P:2 * P], ident[:])
                            last.then_inc(full, 1)
                    else:
                        if at in (H_AT[1], H_AT[3]) and B.has(1):
                            hidden(H_AT.index(at))
                        if at == (1, 3) and B.has(-1):
                            claim("PR")
                            taken_out("AT")
                            for t in range(NT):
                                last = mm(work[:, P * t:P * t + P], attT[:, P * t:P * t + P], wproj[:],
                                          start=True, stop=True)
                            last.then_inc(full, 1)
                        if at in (Q_AT[1], K_AT[1]) and B.has(2):
                            side = kt - Q_AT[1][1]
                            claim(("QT", "KT")[side])
                            if side == 0:
                                taken_out("XT")
                            mm(work[:], wqkv[:, P * side:P * side + P], xnT[:, B.parity(2), 1:T + 1],
                               start=True, stop=True).then_inc(full, 1)

                def late(u, kt):
                    at, full = (u, kt), s["work_full"]
                    if layer == 0:
                        if at == (0, 1) and B.has(1):
                            channel_mix("FR", 0)
                        if at == (1, 0) and B.has(1):
                            claim("FV")
                            pe.wait_ge(s["kact_done"], B.count(1, 1, 1))
                            mm(work[:], wrkv[:, 2, :], fd[:], start=True, stop=True).then_inc(full, 1)
                        if at in (PJ_AT[0], PJ_AT[3]) and B.has(2):
                            project(PJ_AT.index(at))
                    else:
                        if at in (H_AT[0], H_AT[2]) and B.has(1):
                            hidden(H_AT.index(at))
                        if at == (1, 1) and B.has(-1):
                            claim("AT")
                            taken_out("OT1")
                            for t in range(NT):
                                last = tr(work[:, P * t:P * t + P], att[:, t, :], ident[:])
                            last.then_inc(full, 1)
                        if at == (2, 0) and B.has(1):
                            claim("VP")
                            for t in range(NT):
                                last = mm(work[:, P * t:P * t + P],
                                          xnT[:, B.parity(1), 1 + P * t:1 + P * t + P], wqkv[:, 2 * P:3 * P],
                                          start=True, stop=True)
                            last.then_inc(full, 1)
                        if at == (2, 1) and B.has(1):
                            claim("Y")
                            taken_out("H3")
                            for t in range(NT):
                                for f in range(NF):
                                    last = mm(work[:, P * t:P * t + P], big[:, f, P * t:P * t + P], w2[:, f, :],
                                              start=(f == 0), stop=(f == NF - 1))
                            last.then_inc(full, 1)

                def channel_mix(name, n):
                    claim(name)
                    pe.wait_ge(s["mix_done"], B.count(4, 2 * n + 2, 1))
                    mm(work[:], wrkv[:, n, :], (fa, fb)[n][:], start=True, stop=True).then_inc(s["work_full"], 1)

                def project(t):
                    claim(f"PJ{t}")
                    if t == 0:
                        taken_out("XT")
                    mm(work[:], xnT[:, B.parity(2), 1 + P * t:1 + P * t + P], wcat[:].rearrange("p a n -> p (a n)"),
                       start=True, stop=True).then_inc(s["work_full"], 1)

                def hidden(f):
                    claim(f"H{f}")
                    mm(work[:], w1[:, P * f:P * f + P], xnT[:, B.parity(1), 1:T + 1],
                       start=True, stop=True).then_inc(s["work_full"], 1)

                for u in range(NG):
                    for kt in range(NT):
                        pvo, pu = (-1, NG - 1) if u == 0 else (0, u - 1)
                        if B.has(pvo):
                            pv(pvo, pu, kt)
                        early(u, kt)
                        so, su = (0, u + 2) if u < 2 else (1, u - 2)
                        for j in range(NT):
                            if B.has(0):
                                scores_t(u, kt, j)
                            if B.has(so):
                                scores_max(so, su, kt, j)
                            if j == 1:
                                late(u, kt)

            for layer in range(2):
                run_bodies(pe, layer, body)
                border(pe, 2 + layer)

        @block.scalar
        def _(act):
            fn = nc.scalar.activation
            act.wait_ge(setup_dve, 4)
            for l in range(2):
                fn(lall[:, l, :], lall[:, l, :], ACT.Exp, bias=lst[:, l, 1:2], accum_out=lst[:, l, 2:3])
                fn(lcol[:, l, :], lcol[:, l, :], ACT.Exp, bias=lst[:, l, 1:2]).then_inc(setup_act, 1)
            border(act, 1)

            def body(B):
                s, layer = S[B.layer], B.layer

                full, taken = s["work_full"], s["work_taken"]

                def filled(name):
                    act.wait_ge(full, B.use(name) + 1)

                def early(u, kt):
                    at = (u, kt)
                    mo, mu_ = (u + 1) // NG, (u + 1) % NG
                    if kt == 1 and B.has(mo):
                        filled(f"MT{u}")
                        wait(act, s["mrow_loaded"], B.count(NG * 32, 32 * mu_, mo))
                        fn(mT[:], work[0:2 * G * NT, 0:P // 2].bitcast(BF16), ACT.Copy).then_inc(taken, 1)
                    if at == (0, 3) and B.has(2):
                        filled("XT")
                        fn(xnT[:, B.parity(2), 1:T + 1], work[:], ACT.Copy).then_inc(taken, 1)
                    if at == (Q_AT[layer]) and B.has(2):
                        first_part(0)
                    if at == (K_AT[layer]) and B.has(2):
                        first_part(1)
                    if layer == 0:
                        if at == (0, 2) and B.has(1):
                            filled("FK")
                            fn(fd[:], work[:], ACT.Relu).then_inc(taken, 1)
                        if at in PJ_AT[1:3] and B.has(2):
                            projected(PJ_AT.index(at))
                        if at == (1, 0) and B.has(1):
                            wait(act, s["pv_done"], B.count(NG * NT, 0))
                            fn(vals[:, B.parity(1), :, :, 0:HD],
                               big[:, :, 3 * P:4 * P].rearrange("p t (h d) -> p t h d", h=H), ACT.Copy
                               ).then_inc(s["vals_done"], 1)
                        if at == (2, 2) and B.has(1):
                            filled("FT")
                            if B.has(-1):
                                act.wait_ge(s["post"], B.count(2, 2, -1))
                            fn(ffn[:, B.parity(1)].rearrange("p t d -> p (t d)"), work[:], ACT.Copy, scale=0.5
                               ).then_inc(taken, 1)
                        if at == (3, 0) and B.has(2):
                            act.wait_ge(s["rms"], B.count(4, 3, 2))
                            fn(rrms[:], ssq[:], ACT.Sqrt).then_inc(s["root_done"], 1)
                    elif at in (H_AT[1], H_AT[3]) and B.has(1):
                        hidden(H_AT.index(at))

                def late(u, kt):
                    at = (u, kt)
                    if layer == 0:
                        if at == (0, 1) and B.has(1):
                            filled("FR")
                            fn(fc[:], work[:], ACT.Tanh, scale=0.5).then_inc(taken, 1)
                        if at in (PJ_AT[0], PJ_AT[3]) and B.has(2):
                            projected(PJ_AT.index(at))
                        if at == (2, 0) and B.has(2):
                            act.wait_ge(taken, B.use("PJ3") + 1)
                            fn(sqr[:], big[:, :, 0:2 * P], ACT.Square).then_inc(s["sq_done"], 1)
                    else:
                        if at in (H_AT[0], H_AT[2]) and B.has(1):
                            hidden(H_AT.index(at))
                        if at == (1, 1) and B.has(-1):
                            filled("AT")
                            fn(attT[:], work[:], ACT.Copy).then_inc(taken, 1)
                        if at == (2, 0) and B.has(1):
                            filled("VP")
                            wait(act, s["pv_done"], B.count(NG * NT, 0))
                            fn(vals[:, B.parity(1), :, :, 0:HD].rearrange("p t h d -> p (t h) d"),
                               work[:].rearrange("p (x d) -> p x d", d=HD), ACT.Copy).then_inc(taken, 1)
                        if at == (2, 1) and B.has(1):
                            filled("Y")
                            if B.has(-1):
                                act.wait_ge(s["post"], B.count(2, 2, -1))
                            fn(ffn[:, B.parity(1)].rearrange("p t d -> p (t d)"), work[:], ACT.Copy
                               ).then_inc(taken, 1)

                def first_part(side):
                    filled(("QT", "KT")[side])
                    wait(act, s["parts_stored"], B.count(32, 0, 2))
                    fn(parts[:, side, 0, :], work[:], ACT.Copy).then_inc(s["part0_done"], 1)

                def second_part(side):
                    act.wait_ge(taken, B.use(("QT", "KT")[side]) + 1)
                    fn(parts[:, side, 1, :], rest[:, side], ACT.Copy).then_inc(s["part1_done"], 1)

                def projected(t):
                    filled(f"PJ{t}")
                    if t == 0:
                        wait(act, s["vals_done"], B.count(1, 0, 2))
                    fn(big[:, t, :], work[:], ACT.Copy).then_inc(taken, 1)

                def hidden(f):
                    filled(f"H{f}")
                    fn(fa[:], work[:], ACT.Square, scale=GELU_K ** 0.5).then_inc(s["sq_done"], 1)

                def hidden_tanh(f):
                    act.wait_ge(s["gelu"], B.count(NF, f + 1, 1))
                    fn(fc[:], fb[:], ACT.Tanh, scale=GELU_C).then_inc(s["tanh_done"], 1)

                for u in range(NG):
                    for kt in range(NT):
                        early(u, kt)
                        for j in range(G):
                            if B.has(0):
                                q0 = P * kt if layer == 0 else 0
                                if j == 0:
                                    wait(act, s["pv_done"], B.count(NG * NT, NT * (u - 1) + kt + 1))
                                act.wait_ge(s["st_ready"], B.count(64, 16 * u + 4 * kt + j + 1))
                                fn(probs[:, kt, j, 0:T - q0], st[:, j % 2, 0:T - q0], ACT.Exp,
                                   scale=SCALE).then_inc(s["exp_done"], 1)
                            eo, eu = (-1, NG - 1) if u == 0 else (0, u - 1)
                            if j == 2 and kt == NT - 1 and B.has(eo):
                                act.wait_ge(s["pv_done"], B.count(NG * NT, NT * eu + NT, eo))
                                if B.has(-1 if u < 2 else 0):
                                    filled(f"OT{u}")
                                fn(accS[:], acc[:], ACT.Copy).then_inc(s["acc_taken"], 1)
                            if j == 1:
                                late(u, kt)
                            if j == 1 and (u, kt) == Q_AT[layer] and B.has(2):
                                second_part(0)
                            if j == 1 and (u, kt) == K_AT[layer] and B.has(2):
                                second_part(1)
                            if layer == 1 and B.has(1):
                                if j == 1 and (u, kt) in (H_AT[1], H_AT[3]):
                                    hidden_tanh(H_AT.index((u, kt)))
                                if j == 3 and (u, kt) in (H_AT[0], H_AT[2]):
                                    hidden_tanh(H_AT.index((u, kt)))

            for layer in range(2):
                run_bodies(act, layer, body)
                border(act, 2 + layer)

        @block.vector
        def _(dve):
            v = nc.vector
            dve.wait_ge(setup_in, 16 * SETUP_LOADS)
            v.tensor_copy(causalb[:], causal[:])
            v.tensor_copy(identb[:], ident[:]).then_inc(setup_dve, 1)
            for n in range(6):
                rows = P if n in (2, 3) else 64
                last = v.tensor_copy(rep[0:rows, n], small[0:rows, n, :].unsqueeze(1).broadcast_to([rows, H, HD]))
            last.then_inc(setup_dve, 1)
            dve.wait_ge(setup_pe, 1)
            v.tensor_copy(rep[:, 6], work[:, 0:HD].unsqueeze(1).broadcast_to([P, H, HD])).then_inc(setup_dve, 1)
            for l in range(2):
                last = v.reduce_max(lst[:, l, 0:1], lall[:, l, :], AX_X)
            last.then_inc(rep_chain, 1)
            dve.wait_ge(rep_chain, 1)
            for l in range(2):
                last = v.tensor_scalar(lst[:, l, 1:2], lst[:, l, 0:1], -1.0, None, ALU.mult)
            last.then_inc(setup_dve, 1)
            dve.wait_ge(setup_act, 2)
            for l in range(2):
                last = v.reciprocal(lst[:, l, 3:4], lst[:, l, 2:3])
            last.then_inc(rep_chain, 1)
            dve.wait_ge(rep_chain, 2)
            for l in range(2):
                last = v.tensor_scalar(lcol[:, l, :], lcol[:, l, :], lst[:, l, 3:4], None, ALU.mult)
            last.then_inc(rep_chain, 1)
            dve.wait_ge(rep_chain, 3)
            for l, stage in ((0, stage_a1), (1, stage_b2)):
                dve.wait_ge(compose_in[3 * l], 16)
                rows = stage.rearrange("p (c n) -> p c n", c=NC)
                v.tensor_tensor(rows, rows, lcol[:, l, :].unsqueeze(2).broadcast_to([P, NC, P]),
                                ALU.mult).then_inc(setup_dve, 1)
            dve.wait_ge(setup_pe, 2)
            v.tensor_tensor(wcat[:], s1[:, 0, :].rearrange("p (a n) -> p a n", a=4),
                            blocks[:].unsqueeze(1).broadcast_to([P, 4, P]), ALU.mult)
            v.tensor_tensor(normw[:, 1, :], normw[:, 0, :], normw[:, 1, :], ALU.mult).then_inc(rep_chain, 1)
            dve.wait_ge(rep_chain, 4)
            other = wcat[:, 2, :].rearrange("p (h d) -> p h d", h=H)
            v.tensor_tensor(other, other, normw[:, 0, :].unsqueeze(1).broadcast_to([P, H, HD]), ALU.mult)
            v.tensor_scalar(mu[:, 2:4], mu[:, 0:2], -1.0, 1.0, ALU.mult, ALU.add)
            v.memset(xnT[:, :, 0:1], 0.0)
            dve.wait_ge(setup_pe, 3)
            v.tensor_copy(w1[:], st[:, 0, :])
            dve.wait_ge(setup_pe, 4)
            v.tensor_scalar(w2[:].rearrange("p f d -> p (f d)"), st[:, 1, :], 0.5, None, ALU.mult)
            v.memset(stacks[:, 0].rearrange("p s n -> p (s n)").bitcast(mybir.dt.uint32), 0)
            v.memset(vals[:], 0.0).then_inc(rep_chain, 1)
            dve.wait_ge(rep_chain, 5)
            v.memset(stacks[MROW:KROWS, 0, 1, :], 1.0)
            v.memset(vals[:, :, :, :, HD:HD + 1].rearrange("p a t h d -> p (a t h) d"), 1.0)
            border(dve, 1)

            def body(B):
                s, layer = S[B.layer], B.layer

                full, taken = s["work_full"], s["work_taken"]

                def filled(name):
                    dve.wait_ge(full, B.use(name) + 1)

                def taken_out(name):
                    dve.wait_ge(taken, B.use(name) + 1)

                def link(op, name, per, n, off):
                    op.then_inc(s[name], 1)
                    dve.wait_ge(s[name], B.count(per, n, off))

                def early(u, kt):
                    at = (u, kt)
                    mo, mu_ = (u + 1) // NG, (u + 1) % NG
                    if kt == 0 and B.has(mo):
                        m = maxs[:, mu_ % 2, :]
                        dve.wait_ge(s["red_done"], B.count(64, 16 * mu_ + 16, mo))
                        link(v.tensor_scalar(msp[:, 0, :], m, -1.0, None, ALU.mult),
                             "msplit", 2 * NG, 2 * mu_ + 1, mo)
                        v.scalar_tensor_tensor(out=msp[:, 1, :], in0=m, scalar=-1.0, in1=msp[:, 0, :],
                                               op0=ALU.mult, op1=ALU.subtract).then_inc(s["msplit"], 1)
                    oo, ou = (-1, u + 2) if u < 2 else (0, u - 2)
                    if kt == 0 and B.has(oo):
                        filled(f"OT{u}")
                        heads = work[:].rearrange("p (t j c) -> p t j c", t=NT, j=G)
                        link(v.reciprocal(rsum[:], heads[:, :, :, HD]), "rec", NG, ou + 1, oo)
                        if ou == 0 and layer == 0 and B.has(oo - 1):
                            dve.wait_ge(s["post"], B.count(2, 2, oo - 1))
                        v.tensor_tensor(
                            att[:, :, G * HD * ou:G * HD * (ou + 1)].rearrange("p t (j d) -> p t j d", j=G),
                            heads[:, :, :, 0:HD], rsum[:].unsqueeze(3).broadcast_to([P, NT, G, HD]),
                            ALU.mult).then_inc(taken, 1)
                    if at == (0, 0) and B.has(2):
                        dve.wait_ge(s["x_loaded"], B.count(16, 16, 2))
                        for t in range(NT):
                            last = v.bn_stats(stats[:, t, :], x_tile[:, t, :])
                        last.then_inc(s["ln"], 1)
                        wait_apart(dve, s["ln"], B.count(3, 1, 2), passed)
                        for t in range(NT):
                            last = v.bn_aggr(mv[:, t, :], stats[:, t, :])
                        link(last, "ln", 3, 2, 2)
                        v.tensor_scalar(mv[:, :, 1], mv[:, :, 1], LN_EPS, None, ALU.add).then_inc(s["ln"], 1)
                    if at == (0, 2) and B.has(2):
                        dve.wait_ge(s["pow_ln"], B.count(1, 1, 2))
                        for t in range(NT):
                            v.tensor_scalar(xn[:, t, :], x_tile[:, t, :], mv[:, t, 0:1], rstd[:, t:t + 1],
                                            ALU.subtract, ALU.mult).then_inc(s["xn_done"], 1)
                    if at == Q_AT[layer] and B.has(2):
                        leave_rest(0)
                    if at == K_AT[layer] and B.has(2):
                        leave_rest(1)
                    if layer == 0:
                        if at == (0, 1) and B.has(1):
                            xt = xnT[:, B.parity(1), :]
                            for n, mix in enumerate((fa, fb)):
                                link(v.tensor_scalar(mix[:], xt[:, 1:T + 1], mu[:, n:n + 1], None, ALU.mult),
                                     "mix_done", 4, 2 * n + 1, 1)
                                v.scalar_tensor_tensor(out=mix[:], in0=xt[:, 0:T], scalar=mu[:, 2 + n:3 + n],
                                                       in1=mix[:], op0=ALU.mult, op1=ALU.add
                                                       ).then_inc(s["mix_done"], 1)
                        if at == (2, 2) and B.has(2):
                            dve.wait_ge(s["sq_done"], B.count(1, 1, 2))
                            link(v.reduce_sum(ssq[:].rearrange("p (t x) -> p t x", t=NT),
                                              sqr[:].rearrange("p t (x d) -> p t x d", d=HD), AX_X),
                                 "rms", 4, 1, 2)
                            link(v.tensor_scalar(ssq[:], ssq[:], 1.0 / HD, RMS_EPS, ALU.mult, ALU.add),
                                 "rms", 4, 2, 2)
                            v.reciprocal(ssq[:], ssq[:]).then_inc(s["rms"], 1)
                        if at == (3, 1) and B.has(2):
                            dve.wait_ge(s["root_done"], B.count(1, 1, 2))
                            qk = big[:, :, 0:2 * P].rearrange("p t (x d) -> p t x d", d=HD)
                            v.tensor_tensor(qk, qk, rrms[:].rearrange("p (t x) -> p t x", t=NT)
                                            .unsqueeze(3).broadcast_to([P, NT, 2 * H, HD]), ALU.mult
                                            ).then_inc(s["rms"], 1)
                    else:
                        if at in (H_AT[1], H_AT[3]) and B.has(1):
                            gelu_inner(H_AT.index(at))
                        if at == (1, 3) and B.has(-1):
                            filled("PR")
                            dve.wait_ge(s["res_loaded"], B.count(16, 16, -1))
                            wait(dve, s["x_stored"], B.count(16, 0, -1))
                            v.tensor_tensor(x_new[:].rearrange("p t d -> p (t d)"), work[:],
                                            x_res[:].rearrange("p t d -> p (t d)"), ALU.add).then_inc(taken, 1)
                            taken_out("PR")
                            link(v.tensor_tensor(x_new[:], x_new[:], ffn[:, B.parity(-1)], ALU.add),
                                 "post", 2, 1, -1)
                            v.tensor_tensor(x_new[:], x_new[:], bproj[:].unsqueeze(1).broadcast_to([P, NT, D]),
                                            ALU.add).then_inc(s["post"], 1)

                def late(u, kt):
                    at = (u, kt)
                    if layer == 0:
                        if at == (1, 0) and B.has(1):
                            filled("FV")
                            v.scalar_tensor_tensor(out=fa[:], in0=fc[:], scalar=1.0, in1=work[:],
                                                   op0=ALU.add, op1=ALU.mult).then_inc(taken, 1)
                    else:
                        if at in (H_AT[0], H_AT[2]) and B.has(1):
                            gelu_inner(H_AT.index(at))

                def leave_rest(side):
                    filled(("QT", "KT")[side])
                    dve.wait_ge(s["part0_done"], B.count(2, side + 1, 2))
                    v.tensor_tensor(rest[:, side], work[:], parts[:, side, 0, :], ALU.subtract).then_inc(taken, 1)

                def third_part(side):
                    dve.wait_ge(s["part1_done"], B.count(2, side + 1, 2))
                    v.tensor_tensor(parts[:, side, 2, :], rest[:, side], parts[:, side, 1, :],
                                    ALU.subtract).then_inc(s["part2_done"], 1)

                def gelu_inner(f):
                    filled(f"H{f}")
                    dve.wait_ge(s["sq_done"], B.count(NF, f + 1, 1))
                    v.scalar_tensor_tensor(out=fb[:], in0=fa[:], scalar=1.0, in1=work[:], op0=ALU.add,
                                           op1=ALU.mult).then_inc(s["gelu"], 1)

                def gelu_outer(f):
                    dve.wait_ge(s["tanh_done"], B.count(NF, f + 1, 1))
                    v.scalar_tensor_tensor(out=big[:, f, :], in0=fc[:], scalar=1.0, in1=work[:],
                                           op0=ALU.add, op1=ALU.mult).then_inc(taken, 1)

                for u in range(NG):
                    for kt in range(NT):
                        early(u, kt)
                        so, su = (0, u + 2) if u < 2 else (1, u - 2)
                        for j in range(NT):
                            m = NT * kt + j
                            if B.has(so) and layer == 0:
                                dve.wait_ge(s["s1_ready"], B.count(64, 16 * su + m + 1, so))
                                v.reduce_max(maxs[:, su % 2, m:m + 1], s1[:, j, 0:P * (j + 1)], AX_X
                                             ).then_inc(s["red_done"], 1)
                            if B.has(so) and layer == 1 and j % 2 == 1:
                                dve.wait_ge(s["s1_ready"], B.count(64, 16 * su + m + 1, so))
                                v.reduce_max(maxs[:, su % 2, m - 1:m + 1], s1[:, j - 1:j + 1, :], AX_X
                                             ).then_inc(s["red_done"], 2)
                            pvo, pu = (-1, NG - 1) if u == 0 else (0, u - 1)
                            if layer == 1 and kt == 1 and j >= POOL_HEADS and B.has(pvo):
                                dve.wait_ge(s["exp_done"], B.count(64, 16 * pu + 16, pvo))
                                last = v.tensor_tensor(probs[:, 3, j, :], probs[:, 3, j, :], ebias[:, 3, :], ALU.mult)
                                if j == G - 1:
                                    last.then_inc(s["emul_dve"], 1)
                            if j == 1:
                                late(u, kt)
                            if layer == 1 and B.has(2) and j == 2:
                                if (u, kt) == Q_AT[1]:
                                    third_part(0)
                                if (u, kt) == K_AT[1]:
                                    third_part(1)
                            if layer == 1 and B.has(1):
                                if j == 2 and (u, kt) in (H_AT[1], H_AT[3]):
                                    gelu_outer(H_AT.index((u, kt)))
                                if j == 3 and (u, kt) in (H_AT[0], H_AT[2]):
                                    gelu_outer(H_AT.index((u, kt)))

            for layer in range(2):
                run_bodies(dve, layer, body)
                border(dve, 2 + layer)

        @block.gpsimd
        def _(pool):
            g = nc.gpsimd
            g.memset(half[:], -0.5)
            g.memset(stacks[:, 1].rearrange("p s n -> p (s n)"), 0.0).then_inc(setup_pool, 1)
            pool.wait_ge(setup_pool, 1)
            g.memset(stacks[MROW:KROWS, 1, 1, :], 1.0)
            border(pool, 1)

            def body(B):
                s, layer = S[B.layer], B.layer

                def third_part(side):
                    pool.wait_ge(s["part1_done"], B.count(2, side + 1, 2))
                    g.tensor_tensor(parts[:, side, 2, :], rest[:, side], parts[:, side, 1, :],
                                    ALU.subtract).then_inc(s["part2_done"], 1)

                for u in range(NG):
                    for kt in range(NT):
                        at = (u, kt)
                        if at == (0, 0) and B.has(2):
                            pool.wait_ge(s["ln"], B.count(3, 3, 2))
                            g.tensor_tensor(rstd[:], mv[:, :, 1], half[:, 0:NT], ALU.pow).then_inc(s["pow_ln"], 1)
                        if layer == 0 and at == (0, 2) and B.has(1):
                            pool.wait_ge(s["work_taken"], B.use("FK") + 1)
                            g.tensor_tensor(fd[:], fd[:], fd[:], ALU.mult).then_inc(s["kact_done"], 1)
                        if layer == 0 and at == (1, 1) and B.has(-1):
                            pool.wait_ge(s["work_taken"], B.use("OT1") + 1)
                            pool.wait_ge(s["res_loaded"], B.count(16, 16, -1))
                            wait(pool, s["x_stored"], B.count(16, 0, -1))
                            g.tensor_tensor(x_new[:], x_res[:], att[:], ALU.add).then_inc(s["post"], 1)
                            pool.wait_ge(s["post"], B.count(2, 1, -1))
                            g.tensor_tensor(x_new[:], x_new[:], ffn[:, B.parity(-1)], ALU.add
                                            ).then_inc(s["post"], 1)
                        if layer == 0 and at == (3, 1) and B.has(2):
                            pool.wait_ge(s["rms"], B.count(4, 4, 2))
                            k = big[:, :, P:2 * P]
                            kh = k.rearrange("p t (h d) -> p t h d", h=H)
                            g.tensor_tensor(kh, kh, normw[:, 1, :].unsqueeze(1).unsqueeze(1)
                                            .broadcast_to([P, NT, H, HD]), ALU.mult).then_inc(s["k_done"], 1)
                            pool.wait_ge(s["k_done"], B.count(2, 1, 2))
                            g.tensor_tensor(k, k, big[:, :, 2 * P:3 * P], ALU.add).then_inc(s["k_done"], 1)
                        if B.has(0) and layer == 0:
                            wait_apart(pool, s["exp_done"], B.count(64, 16 * u + 4 * kt + 4), passed)
                            diag = probs[:, kt, :, 0:P]
                            g.affine_select(out=diag, in_=diag, compare_op=ALU.is_ge, fill=0.0, base=0,
                                            pattern=[[0, G], [1, P]], channel_multiplier=-1
                                            ).then_inc(s["masked"], 1)
                        if layer == 0 and at == Q_AT[0] and B.has(2):
                            third_part(0)
                        if layer == 0 and at == K_AT[0] and B.has(2):
                            third_part(1)
                        if B.has(0) and layer == 1:
                            n = G if kt < NT - 1 else POOL_HEADS
                            pool.wait_ge(s["exp_done"], B.count(64, 16 * u + 4 * kt + 4))
                            g.tensor_tensor(probs[:, kt, 0:n], probs[:, kt, 0:n],
                                            ebias[:, kt, :].unsqueeze(1).broadcast_to([P, n, T]), ALU.mult
                                            ).then_inc(s["emul_pool"], 1)

            for layer in range(2):
                run_bodies(pool, layer, body)
                border(pool, 2 + layer)


def kernel(**inputs):
    import numpy as _np
    import concourse.bacc as _bacc
    from concourse import mybir as _mybir
    from concourse.bass_utils import run_bass_kernel_spmd as _run

    f = {k: _np.asarray(v) for k, v in inputs.items()}
    send = {k: f[k] for k in ("L0_attn_x", "L0_attn_W_DQ", "L0_attn_W_DKV", "L0_attn_W_UKV", "L0_attn_W_QR",
                              "L0_attn_W_KR", "L0_attn_q_norm_w", "L0_attn_k_norm_w", "L1_attn_w_qkv",
                              "L1_attn_w_proj", "L1_attn_b_proj", "L1_ffn_fc1_logits", "L1_ffn_fc2_logits")}
    send["W_UQ_T"] = f["L0_attn_W_UQ"].T
    send["W_UKV_K_T"] = f["L0_attn_W_UKV"][:HD].T
    send["W_O_T"] = f["L0_attn_W_O"].T
    send["W_r_T"] = f["L0_ffn_W_r"].T
    send["W_k_T"] = f["L0_ffn_W_k"].T
    send["W_v_T"] = f["L0_ffn_W_v"].T
    send["mu_r"] = f["L0_ffn_mu_r"].reshape(P, 1)
    send["mu_k"] = f["L0_ffn_mu_k"].reshape(P, 1)
    send["fc1_A_T"] = f["L1_ffn_fc1_A"].transpose(0, 2, 1).reshape(NC * P, D)
    send["fc1_B"] = f["L1_ffn_fc1_B"].reshape(NC * P, FF)
    send["fc2_A_T"] = f["L1_ffn_fc2_A"].transpose(0, 2, 1).reshape(NC * P, FF)
    send["fc2_B"] = f["L1_ffn_fc2_B"].reshape(NC * P, D)
    n = _np.arange(P)
    send["ident"] = _np.eye(P, dtype=_np.float32)
    send["causal"] = _np.where(n[None, :] > n[:, None], NEG, 0.0).astype(_np.float32)
    send["blocks"] = (n[None, :] // HD == n[:, None] // HD).astype(_np.float32)
    pos = _np.mod(_np.arange(T, dtype=_np.float32) * _np.float32((1.0 + _np.sqrt(5.0)) / 2.0), _np.float32(1.0))
    send["ebias"] = (_np.exp(-_np.abs(pos[:, None] - pos[None, :])) + _np.float32(1e-8)).astype(_np.float32)

    nc = _bacc.Bacc("TRN2", target_bir_lowering=False, num_devices=1)
    arrays, args = {}, {}
    for name, value in send.items():
        value = _np.ascontiguousarray(value)
        arrays[f"in_{name}_dram"] = value
        args[name] = nc.dram_tensor(f"in_{name}_dram", value.shape, _mybir.dt.from_np(value.dtype),
                                    kind="ExternalInput").ap()
    out = nc.dram_tensor("out_0_dram", (NB, T, D), _mybir.dt.float32, kind="ExternalOutput").ap()
    build(nc, args, out)
    r = _run(nc, [arrays], core_ids=[0])
    return r.results[0]["out_0_dram"]
```

```python
from contextlib import ExitStack
from itertools import zip_longest

import concourse.bass as bass
from concourse import mybir

F32 = mybir.dt.float32
BF16 = mybir.dt.bfloat16
ALU = mybir.AluOpType
ACT = mybir.ActivationFunctionType
AX_X = mybir.AxisListType.X

P = 128
NB, T, D = 16, 512, 128
H, HD = 16, 8
NT = T // P
G = 4
NG = H // G
FF = 512
NF = FF // P
PRIM, RANK = 32, 64
NC = PRIM * RANK // P
VW = 32
SCALE = float(HD) ** -0.5
LN_EPS = 1e-5
RMS_EPS = 1.1920929e-07
NEG = -1e30
GELU_C, GELU_K = 0.7978845608028654, 0.044715

Q_PARTS = (0, 0, 1, 0, 1, 2)
K_PARTS = (0, 1, 0, 2, 1, 0)
TERMS = len(Q_PARTS)
POOL_HEADS = (1, 2, 1, 2)
MROW = 96
KROWS = MROW + 2
FIRST, LAST = -2, NB
COMPOSE_FROM = 24
STEADY, PAIRS = 2, 6

PACKS = {
    0: (((0, 0),), ((2, 0), (2, 1)), ((0, 1),), ((1, 0), (3, 0)), ((0, 2),), ((1, 1), (3, 1)), ((0, 3),),
        ((2, 2), (2, 3)), ((1, 2), (3, 2)), ((1, 3), (3, 3))),
    1: tuple(((kt, j),) for kt in range(NT) for j in range(G)),
}
TILES = [[(p, pack, tile) for p, pack in enumerate(PACKS[layer]) for tile in pack] for layer in range(2)]
PACK_ROWS = len(PACKS[0])
EXPS = [len(PACKS[layer]) for layer in range(2)]


def place(layer, kt, j):
    if layer == 1:
        return G * kt + j, 0, T
    width = T - P * kt
    row, column = {0: (j, 0), 1: (G + j, 0), 3: (G + j, T - P), 2: (2 * G + j // 2, 2 * P * (j % 2))}[kt]
    return row, column, width


WORK_USES = {
    0: {"OT0": (1, 0, -1), "MT0": (4, 0, 0), "FR": (6, 1, 1), "FK": (8, 0, 1), "FV": (13, 0, 1),
        "OT1": (16, 0, -1), "XT": (19, 0, 2), "MT1": (20, 0, 0), "PJ0": (22, 0, 2), "PJ1": (24, 1, 2),
        "PJ2": (28, 0, 2), "PJ3": (31, 0, 2), "OT2": (34, 0, 0), "MT2": (37, 2, 0), "FT": (40, 0, 1),
        "QT": (46, 0, 2), "OT3": (49, 0, 0), "KT": (51, 0, 2), "MT3": (57, 1, 1)},
    1: {"OT0": (0, 0, -1), "H0": (3, 0, 1), "MT0": (4, 2, 0), "H1": (9, 0, 1), "H2": (15, 0, 1),
        "MT1": (17, 0, 0), "OT1": (18, 0, -1), "XT": (20, 0, 2), "H3": (24, 1, 1), "AT": (28, 0, -1),
        "PR": (30, 0, -1), "VP": (32, 0, 1), "MT2": (34, 1, 0), "OT2": (36, 0, 0), "QT": (39, 0, 2),
        "KT": (44, 1, 2), "OT3": (49, 0, 0), "MT3": (53, 1, 1), "Y": (57, 5, 1)},
}
OTHER_WORK = {
    0: {"MIX": (0, 1), "LN": (4, 2), "NORM": (7, 2), "VALUES": (15, 1), "POST": (21, -1),
        "SQUARE": (32, 2), "MEAN": (34, 2), "ROOT": (38, 2), "SCALE_QK": (43, 2)},
    1: {"LN": (4, 2), "NORM": (16, 2)},
}
USES = [sorted(((n, use[2]) for n, use in WORK_USES[layer].items()), key=lambda n: WORK_USES[layer][n[0]][0])
        for layer in range(2)]


class Body:

    def __init__(self, layer, number, i=None):
        self.layer, self.number, self.i = layer, number, i
        self.beside = None

    def has(self, off):
        return 0 <= self.number + off < NB

    def parity(self, off):
        return (self.number + off) % 2

    def due(self, name, slot):
        at = {**WORK_USES[self.layer], **OTHER_WORK[self.layer]}[name]
        return at[0] == slot and self.has(at[-1])

    def out(self, name, slot, more=0):
        at, later, off = WORK_USES[self.layer][name]
        return at + later + more == slot and self.has(off)

    def after(self, name, slot, later):
        at, off = OTHER_WORK[self.layer][name]
        return at + later == slot and self.has(off)

    def count(self, per, extra=0, off=0):
        fixed = per * (self.number + off) + extra
        return fixed if self.i is None else self.i * (2 * per) + fixed

    def use(self, name):
        table = USES[self.layer]
        before = sum(1 for n in range(FIRST, self.number) for _, off in table if 0 <= n + off < NB)
        for n, off in table:
            if n == name:
                break
            before += self.has(off)
        return before if self.i is None else self.i * (2 * len(table)) + before


    def other_layers_uses(self, name):
        other = self.beside
        slot = WORK_USES[self.layer][name][0] + (other.layer == 0)
        table = USES[other.layer]
        before = sum(1 for n in range(FIRST, other.number) for _, off in table if 0 <= n + off < NB)
        return before + sum(1 for n, off in table if WORK_USES[other.layer][n][0] < slot and other.has(off))


def run(body):
    for _ in body:
        pass


def run_first_layer(eng, body):
    for n in range(FIRST + 1, STEADY):
        run(body(Body(0, n)))
    with eng.Fori(0, PAIRS) as i:
        for n in (STEADY, STEADY + 1):
            run(body(Body(0, n, i)))
    for n in range(STEADY + 2 * PAIRS, LAST - 1):
        run(body(Body(0, n)))


def run_both_layers(body, n):
    old, new = Body(0, LAST - 1 + n), Body(1, FIRST + n)
    old.beside, new.beside = new, old
    for _ in zip_longest(body(old), body(new)):
        pass


def run_second_layer(eng, body):
    for n in range(FIRST + 2, STEADY):
        run(body(Body(1, n)))
    with eng.Fori(0, PAIRS) as i:
        for n in (STEADY, STEADY + 1):
            run(body(Body(1, n, i)))
    for n in range(STEADY + 2 * PAIRS, LAST + 1):
        run(body(Body(1, n)))


def wait(eng, sem, value):
    if not isinstance(value, int) or value > 0:
        eng.wait_ge(sem, value)


def wait_apart(eng, sem, value, passed):
    if not isinstance(value, int):
        eng.wait_ge(sem, value)
        eng.sem_inc(passed, 1)
    elif value > 0:
        eng.wait_ge(sem, value)


def build(nc, a, out):
    x_in = a["L0_attn_x"]
    x1_dram = nc.dram_tensor("x1_between_layers", (NB, T, D), F32).ap()
    parts_dram = nc.dram_tensor("parts_scratch", (2, 3, P, T), BF16).ap()
    x_src = {0: x_in, 1: x1_dram}
    x_dst = {0: x1_dram, 1: out}

    with ExitStack() as ctx:
        def sb(name, shape, dt=F32):
            return ctx.enter_context(nc.sbuf_tensor(name, shape, dt))

        def sem(name):
            return ctx.enter_context(nc.semaphore(name))

        s1 = ctx.enter_context(nc.psum_tensor("scores_for_max", [P, NT, T], F32))
        st = ctx.enter_context(nc.psum_tensor("scores_transposed", [P, 2, T], F32))
        acc = ctx.enter_context(nc.psum_tensor("pv_acc", [P, T], F32))
        work = ctx.enter_context(nc.psum_tensor("work", [P, T], F32))

        stacks = sb("stacks", [P, 2, 2, H * T], BF16)
        qs = [stacks[:, p, 0, :].rearrange("p (h n) -> p h n", h=H) for p in range(2)]
        ks = [stacks[:, p, 1, :].rearrange("p (h n) -> p h n", h=H) for p in range(2)]
        probs = sb("probs", [P, 2 * PACK_ROWS, T])
        vals = sb("vals", [P, 2, NT, H, VW])
        big = sb("big", [P, NT, 512])
        parts = sb("parts", [P, 2, 3, T], BF16)
        xnT = sb("xnT", [P, 2, T + 1])
        x_tile = sb("x_tile", [P, NT, D])
        xn = sb("xn", [P, NT, D])
        x_res = sb("x_res", [P, NT, D])
        x_new = sb("x_new", [P, NT, D])
        att = sb("att", [P, NT, H * HD])
        attT = sb("attT", [P, T])
        accS = sb("accS", [P, T])
        ffn = sb("ffn", [P, 2, NT, D])
        rest = sb("rest", [P, 2, T])
        fa = sb("fa", [P, T])
        fb = sb("fb", [P, T])
        fc = sb("fc", [P, T])
        fd = sb("fd", [P, T])
        stats = sb("stats", [P, NT, 6])
        mv = sb("mv", [P, NT, 2])
        rstd = sb("rstd", [P, NT])
        sqr = sb("sqr", [P, NT, 2 * P])
        ssq = sb("ssq", [P, NT * 32])
        rrms = sb("rrms", [P, NT * 32])
        maxs = sb("maxs", [P, 2, G * NT])
        msp = sb("msp", [P, 2, G * NT], BF16)
        mT = sb("mT", [2 * G * NT, P], BF16)
        rsum = sb("rsum", [P, NT, G])
        half = sb("minus_half", [P, NT * 32])
        ident = sb("ident", [P, P])
        identb = sb("identb", [P, P], BF16)
        causal = sb("causal", [P, P])
        causalb = sb("causalb", [P, P], BF16)
        blocks = sb("blocks", [P, P])
        ebias = sb("ebias", [P, NT, T])
        wcat = sb("wcat", [P, 4, P])
        wrkv = sb("wrkv", [P, 3, P])
        mu = sb("mu", [P, 4])
        normw = sb("normw", [P, 2, HD])
        wqkv = sb("wqkv", [P, 3 * P])
        wproj = sb("wproj", [P, P])
        bproj = sb("bproj", [P, P])
        w1 = sb("w1", [P, FF])
        w2 = sb("w2", [P, NF, D])
        small = sb("small", [P, 8, HD])
        ukv_v = sb("ukv_v", [HD, P])
        rep = sb("rep", [P, 7, H, HD])
        lall = sb("lall", [P, 2, PRIM])
        lcol = sb("lcol", [P, 2, NC])
        lst = sb("lst", [P, 2, 4])

        setup_in = sem("setup_in")
        later_in = sem("later_in")
        ones_in = sem("ones_in")
        compose_in = [sem(f"compose_in{i}") for i in range(4)]
        setup_dve = sem("setup_dve")
        setup_act = sem("setup_act")
        setup_pe = sem("setup_pe")
        setup_pool = sem("setup_pool")
        rep_chain = sem("rep_chain")
        passed = sem("passed")
        ready = sem("ready")
        S = []
        for layer in range(2):
            S.append({n: sem(f"{n}_{layer}") for n in (
                "x_loaded", "res_loaded", "parts_stored", "stack_loaded", "mrow_loaded", "x_stored",
                "work_full", "work_taken",
                "st_ready", "s1_ready", "pv_done",
                "exp_done", "acc_taken", "sq_done", "tanh_done", "part0_done", "part1_done", "root_done",
                "vals_done",
                "red_done", "msplit", "ln", "xn_done", "mix_done", "rms", "rest_done",
                "rec", "gelu", "hidden_done", "emul_dve",
                "part2_done", "post",
                "pow_ln", "kact_done", "masked", "emul_pool", "k_done")})

        block = ctx.enter_context(nc.Block())
        ENGINES = 5
        SETUP_LOADS, LATER_LOADS = 19, 9

        def border(eng, n):
            eng.drain().then_inc(ready, 1)
            eng.wait_ge(ready, ENGINES * n)

        stage_b1 = probs[:, 0:NC].rearrange("p a n -> p (a n)")
        stage_a1 = vals[:, 0].rearrange("p a b n -> p (a b n)")
        stage_b2 = vals[:, 1].rearrange("p a b n -> p (a b n)")
        stage_a2 = stacks[:, 0].rearrange("p s n -> p (s n)").bitcast(F32)

        @block.sync
        def _(sp):
            loads = [
                (small[0:64, 0, :], a["L0_attn_W_DQ"]), (small[0:64, 1, :], a["W_UQ_T"]),
                (small[:, 2, :], a["L0_attn_W_DKV"]), (small[:, 3, :], a["W_UKV_K_T"]),
                (small[0:64, 4, :], a["L0_attn_W_KR"]), (small[0:64, 5, :], a["L0_attn_W_QR"]),
                (ukv_v[:], a["L0_attn_W_UKV"][HD:2 * HD, :]), (small[0:HD, 6, :], a["W_O_T"]),
                (ident[:], a["ident"]), (causal[:], a["causal"]), (blocks[:], a["blocks"]),
                (normw[:, 0, :], a["L0_attn_q_norm_w"].unsqueeze(0).broadcast_to([P, HD])),
                (normw[:, 1, :], a["L0_attn_k_norm_w"].unsqueeze(0).broadcast_to([P, HD])),
                (lall[:, 0, :], a["L1_ffn_fc1_logits"].unsqueeze(0).broadcast_to([P, PRIM])),
                (lall[:, 1, :], a["L1_ffn_fc2_logits"].unsqueeze(0).broadcast_to([P, PRIM])),
            ]
            for dst, src in loads:
                sp.dma_start(dst, src).then_inc(setup_in, 16)
            for l, name in enumerate(("L1_ffn_fc1_logits", "L1_ffn_fc2_logits")):
                pairs = a[name].rearrange("(c two) -> two c", two=2)
                for two in range(2):
                    sp.dma_start(lcol[64 * two:64 * two + 64, l, :],
                                 pairs[two:two + 1, :].broadcast_to([64, NC]),
                                 allow_slow_non_contiguous=True).then_inc(setup_in, 16)
            def body(B):
                s, layer = S[B.layer], B.layer

                def load_stack(side):
                    wait_apart(sp, s["parts_stored"], B.count(32, 32, 1), passed)
                    wait_apart(sp, s["st_ready"], B.count(NG * EXPS[layer], 0), passed)
                    dst = (qs, ks)[side][B.parity(1)]
                    for t, part in enumerate((Q_PARTS, K_PARTS)[side]):
                        sp.dma_start(dst[8 * t:8 * t + 8, :, :],
                                     parts_dram[side, part].rearrange("(h d) n -> d h n", d=HD)
                                     ).then_inc(s["stack_loaded"], 16)

                for u in range(NG):
                    if u == 0 and B.has(2):
                        wait_apart(sp, s["xn_done"], B.count(NT, 0, 2), passed)
                        sp.dma_start(x_tile[:], x_src[layer][B.count(1, 2)].rearrange("(t p) f -> p t f", p=P)
                                     ).then_inc(s["x_loaded"], 16)
                    if u == 0 and B.has(-1):
                        wait_apart(sp, s["post"], B.count(2, 0, -1), passed)
                        sp.dma_start(x_res[:], x_src[layer][B.count(1, -1)].rearrange("(t p) f -> p t f", p=P)
                                     ).then_inc(s["res_loaded"], 16)
                    off = (u + 1) // NG
                    nu = (u + 1) % NG
                    if B.has(off):
                        wait_apart(sp, s["work_taken"], B.use(f"MT{u}") + 1, passed)
                        for part in range(2):
                            sp.dma_start(
                                qs[B.parity(off)][MROW + part:MROW + part + 1, G * nu:G * nu + G, :]
                                .rearrange("p j (x n) -> p (j x) n", n=P),
                                mT[16 * part:16 * part + 16, :]).then_inc(s["mrow_loaded"], 16)
                    if u == 0 and B.has(1):
                        load_stack(0)
                        load_stack(1)
                    if u == 1 and B.has(-1):
                        wait_apart(sp, s["post"], B.count(2, 2, -1), passed)
                        sp.dma_start(x_dst[layer][B.count(1, -1)].rearrange("(t p) f -> p t f", p=P),
                                     x_new[:]).then_inc(s["x_stored"], 16)
                    if u == 3 and B.has(2):
                        wait_apart(sp, s["stack_loaded"], B.count(2 * TERMS * 16, 0, 2), passed)
                        for side in range(2):
                            wait_apart(sp, s["part2_done"], B.count(2, side + 1, 2), passed)
                            sp.dma_start(parts_dram[side].rearrange("a f n -> f a n"), parts[:, side]
                                         ).then_inc(s["parts_stored"], 16)
                    yield

            run(body(Body(0, FIRST)))
            sp.wait_ge(setup_pool, 3)
            sp.dma_start(stacks[MROW:KROWS, 0, 1, :], stacks[MROW:KROWS, 1, 1, :]).then_inc(ones_in, 16)
            sp.wait_ge(ones_in, 16)
            border(sp, 1)
            run_first_layer(sp, body)
            old = S[0]
            sp.wait_ge(old["xn_done"], NT * NB)
            sp.wait_ge(old["x_stored"], 16 * (LAST - 2))
            sp.wait_ge(old["stack_loaded"], 2 * TERMS * 16 * NB)
            run_both_layers(body, 0)
            sp.wait_ge(old["st_ready"], NG * EXPS[0] * NB)
            run_both_layers(body, 1)
            sp.wait_ge(old["x_stored"], 16 * NB)
            border(sp, 2)
            run_second_layer(sp, body)
            sp.wait_ge(S[1]["x_stored"], 16 * NB)
            border(sp, 3)

        @block.tensor
        def _(pe):
            mm, tr = nc.tensor.matmul, nc.tensor.transpose
            pe.wait_ge(setup_dve, 2)
            mm(work[:, 0:HD], ukv_v[:], small[0:HD, 6, :], start=True, stop=True).then_inc(setup_pe, 1)
            mm(s1[:, 0, 0:P], rep[0:64, 0].rearrange("p h d -> p (h d)"), rep[0:64, 1].rearrange("p h d -> p (h d)"),
               start=True, stop=True)
            mm(s1[:, 0, P:2 * P], rep[:, 2].rearrange("p h d -> p (h d)"), rep[:, 3].rearrange("p h d -> p (h d)"),
               start=True, stop=True)
            mm(s1[:, 0, 2 * P:3 * P], rep[0:64, 4].rearrange("p h d -> p (h d)"),
               rep[0:64, 5].rearrange("p h d -> p (h d)"), start=True, stop=True)
            pe.wait_ge(setup_dve, 3)
            mm(s1[:, 0, 3 * P:4 * P], rep[:, 2].rearrange("p h d -> p (h d)"), rep[:, 6].rearrange("p h d -> p (h d)"),
               start=True, stop=True).then_inc(setup_pe, 1)

            def compose():
                pe.wait_ge(setup_dve, 5)
                c = 0
                for slot, _ in enumerate(body(Body(0, FIRST))):
                    if slot < COMPOSE_FROM or slot % 2 or c == NC:
                        continue
                    if c == 0:
                        pe.wait_ge(setup_dve, 6)
                        pe.wait_ge(compose_in[1], 16)
                    last = mm(st[:, 0, :], stage_a1[:, P * c:P * c + P], stage_b1[:, FF * c:FF * c + FF],
                              start=(c == 0), stop=(c == NC - 1))
                    c += 1
                last.then_inc(setup_pe, 1)
                pe.wait_ge(setup_dve, 7)
                pe.wait_ge(compose_in[2], 16)
                for f in range(NF):
                    for c in range(NC):
                        last = mm(st[:, 1, P * f:P * f + P], stage_a2[:, FF * c + P * f:FF * c + P * f + P],
                                  stage_b2[:, P * c:P * c + P], start=(c == 0), stop=(c == NC - 1))
                last.then_inc(setup_pe, 1)

            def body(B):
                s, layer = S[B.layer], B.layer

                def claim(name):
                    wait(pe, s["work_taken"], B.use(name))
                    if B.beside:
                        wait(pe, S[B.beside.layer]["work_taken"], B.other_layers_uses(name))

                def taken_out(name):
                    pe.wait_ge(s["work_taken"], B.use(name) + 1)

                def pv(off, pu, kt):
                    if layer == 0:
                        pe.wait_ge(s["masked"], B.count(NG * NT, pu * NT + kt + 1, off))
                    else:
                        pe.wait_ge(s["emul_pool"], B.count(NG * NT, pu * NT + kt + 1, off))
                        if kt == NT - 1:
                            pe.wait_ge(s["emul_dve"], B.count(NG, pu + 1, off))
                    if kt == 0:
                        wait(pe, s["acc_taken"], B.count(NG, pu, off))
                        if pu == 0 and layer == 0:
                            pe.wait_ge(s["vals_done"], B.count(1, 1, off))
                    q0 = P * kt if layer == 0 else 0
                    for j in range(G):
                        row, column, width = place(layer, kt, j)
                        row += PACK_ROWS * (pu % 2) if layer == 0 else 0
                        last = mm(acc[32 * j:32 * j + 32, q0:T], vals[:, B.parity(off), kt, G * pu + j, :],
                                  probs[:, row, column:column + width], start=(kt == 0), stop=(kt == NT - 1),
                                  skip_group_check=True)
                    last.then_inc(s["pv_done"], 1)

                def scores_t(u, i):
                    number, pack, (kt, j) = TILES[layer][i]
                    if i == 0:
                        pe.wait_ge(s["mrow_loaded"], B.count(NG * 32, 32 * u + 32))
                    if (kt, j) == pack[0]:
                        wait(pe, s["exp_done"], B.count(NG * EXPS[layer], EXPS[layer] * u + number - 1))
                    q0 = P * kt if layer == 0 else 0
                    column = place(layer, kt, j)[1]
                    h, p = G * u + j, B.parity(0)
                    last = mm(st[:, number % 2, column:column + T - q0], ks[p][0:KROWS, h, P * kt:P * kt + P],
                              qs[p][0:KROWS, h, q0:T], start=True, stop=True)
                    if (kt, j) == pack[-1]:
                        last.then_inc(s["st_ready"], 1)

                def scores_max(off, su, jh, qt):
                    if su == 0 and jh == 0 and qt == 0:
                        pe.wait_ge(s["stack_loaded"], B.count(2 * TERMS * 16, 2 * TERMS * 16, off))
                    wait(pe, s["red_done"], B.count(64, 16 * su + 4 * jh + qt - 3, off))
                    h, p = G * su + jh, B.parity(off)
                    k1 = P * (qt + 1) if layer == 0 else T
                    last = mm(s1[:, qt, 0:k1], qs[p][0:MROW, h, P * qt:P * qt + P], ks[p][0:MROW, h, 0:k1],
                              start=True, stop=(layer == 1))
                    if layer == 0:
                        last = mm(s1[:, qt, P * qt:k1], identb[:], causalb[:], start=False, stop=True)
                    last.then_inc(s["s1_ready"], 1)

                def other(slot):
                    u, full = slot // 16, s["work_full"]
                    oo, ou = (-1, u + 2) if u < 2 else (0, u - 2)
                    mo, mu_ = (u + 1) // NG, (u + 1) % NG
                    if B.due(f"OT{u}", slot):
                        claim(f"OT{u}")
                        pe.wait_ge(s["acc_taken"], B.count(NG, ou + 1, oo))
                        for qt in range(NT):
                            last = tr(work[:, P * qt:P * qt + P], accS[:, P * qt:P * qt + P], ident[:])
                        last.then_inc(full, 1)
                    if B.due(f"MT{u}", slot):
                        claim(f"MT{u}")
                        pe.wait_ge(s["msplit"], B.count(2 * NG, 2 * mu_ + 2, mo))
                        tr(work[0:2 * G * NT, 0:P // 2].bitcast(BF16), msp[:].rearrange("p a b -> p (a b)"),
                           identb[:]).then_inc(full, 1)
                    if B.due("XT", slot):
                        claim("XT")
                        pe.wait_ge(s["xn_done"], B.count(NT, NT, 2))
                        for t in range(NT):
                            last = tr(work[:, P * t:P * t + P], xn[:, t, :], ident[:])
                        last.then_inc(full, 1)
                    if layer == 0:
                        for n, name in enumerate(("FR", "FK")):
                            if B.due(name, slot):
                                claim(name)
                                pe.wait_ge(s["mix_done"], B.count(4, 2 * n + 2, 1))
                                mm(work[:], wrkv[:, n, :], (fa, fb)[n][:], start=True, stop=True).then_inc(full, 1)
                        if B.due("FV", slot):
                            claim("FV")
                            pe.wait_ge(s["kact_done"], B.count(1, 1, 1))
                            mm(work[:], wrkv[:, 2, :], fd[:], start=True, stop=True).then_inc(full, 1)
                        for t in range(NT):
                            if B.due(f"PJ{t}", slot):
                                claim(f"PJ{t}")
                                if t == 0:
                                    taken_out("XT")
                                mm(work[:], xnT[:, B.parity(2), 1 + P * t:1 + P * t + P],
                                   wcat[:].rearrange("p a n -> p (a n)"), start=True, stop=True).then_inc(full, 1)
                        if B.due("FT", slot):
                            claim("FT")
                            taken_out("FV")
                            for t in range(NT):
                                last = tr(work[:, P * t:P * t + P], fa[:, P * t:P * t + P], ident[:])
                            last.then_inc(full, 1)
                        for side, name in enumerate(("QT", "KT")):
                            if B.due(name, slot):
                                claim(name)
                                if side == 0:
                                    pe.wait_ge(s["rms"], B.count(4, 4, 2))
                                else:
                                    pe.wait_ge(s["k_done"], B.count(2, 2, 2))
                                for t in range(NT):
                                    last = tr(work[:, P * t:P * t + P], big[:, t, P * side:P * side + P], ident[:])
                                last.then_inc(full, 1)
                    else:
                        for f in range(NF):
                            if B.due(f"H{f}", slot):
                                claim(f"H{f}")
                                mm(work[:], w1[:, P * f:P * f + P], xnT[:, B.parity(1), 1:T + 1],
                                   start=True, stop=True).then_inc(full, 1)
                        if B.due("AT", slot):
                            claim("AT")
                            taken_out("OT1")
                            for t in range(NT):
                                last = tr(work[:, P * t:P * t + P], att[:, t, :], ident[:])
                            last.then_inc(full, 1)
                        if B.due("PR", slot):
                            claim("PR")
                            taken_out("AT")
                            for t in range(NT):
                                last = mm(work[:, P * t:P * t + P], attT[:, P * t:P * t + P], wproj[:],
                                          start=True, stop=True)
                            last.then_inc(full, 1)
                        if B.due("VP", slot):
                            claim("VP")
                            for t in range(NT):
                                last = mm(work[:, P * t:P * t + P],
                                          xnT[:, B.parity(1), 1 + P * t:1 + P * t + P], wqkv[:, 2 * P:3 * P],
                                          start=True, stop=True)
                            last.then_inc(full, 1)
                        for t in range(NT):
                            if B.out("Y", slot, t - WORK_USES[1]["Y"][1]):
                                if t == 0:
                                    claim("Y")
                                    pe.wait_ge(s["hidden_done"], B.count(NF, NF, 1))
                                for f in range(NF):
                                    last = mm(work[:, P * t:P * t + P], big[:, f, P * t:P * t + P], w2[:, f, :],
                                              start=(f == 0), stop=(f == NF - 1))
                                if t == NT - 1:
                                    last.then_inc(full, 1)
                        for side, name in enumerate(("QT", "KT")):
                            if B.due(name, slot):
                                claim(name)
                                if side == 0:
                                    taken_out("XT")
                                mm(work[:], wqkv[:, P * side:P * side + P], xnT[:, B.parity(2), 1:T + 1],
                                   start=True, stop=True).then_inc(full, 1)

                for u in range(NG):
                    for kt in range(NT):
                        pvo, pu = (-1, NG - 1) if u == 0 else (0, u - 1)
                        if B.has(pvo):
                            pv(pvo, pu, kt)
                        so, su = (0, u + 2) if u < 2 else (1, u - 2)
                        for j in range(NT):
                            if B.has(0):
                                scores_t(u, 4 * kt + j)
                            if B.has(so):
                                scores_max(so, su, kt, j)
                            other(16 * u + 4 * kt + j)
                            yield

            compose()
            border(pe, 1)
            run_first_layer(pe, body)
            run_both_layers(body, 0)
            pe.wait_ge(S[0]["red_done"], 64 * NB)
            run_both_layers(body, 1)
            border(pe, 2)
            run_second_layer(pe, body)
            border(pe, 3)

        @block.scalar
        def _(act):
            fn = nc.scalar.activation
            later_loads = [
                (wrkv[:, 0, :], a["W_r_T"]), (wrkv[:, 1, :], a["W_k_T"]), (wrkv[:, 2, :], a["W_v_T"]),
                (mu[:, 0:1], a["mu_r"]), (mu[:, 1:2], a["mu_k"]),
                (wqkv[:], a["L1_attn_w_qkv"]), (wproj[:], a["L1_attn_w_proj"]),
                (bproj[:], a["L1_attn_b_proj"].unsqueeze(0).broadcast_to([P, D])),
                (ebias[:], a["ebias"].rearrange("(t p) n -> p t n", p=P)),
            ]
            compose_loads = [(stage_a1, "fc1_A_T"), (stage_b1, "fc1_B"), (stage_a2, "fc2_A_T"), (stage_b2, "fc2_B")]

            def load_for_compose(n):
                stage, name = compose_loads[n]
                act.dma_start(stage.rearrange("p (c n) -> p c n", c=NC),
                              a[name].rearrange("(c p) n -> p c n", p=P)).then_inc(compose_in[n], 16)

            act.wait_ge(setup_in, 16 * SETUP_LOADS)
            load_for_compose(0)
            load_for_compose(1)
            for dst, src in later_loads:
                act.dma_start(dst, src).then_inc(later_in, 16)
            load_for_compose(2)
            load_for_compose(3)
            act.wait_ge(setup_dve, 4)
            for l in range(2):
                fn(lall[:, l, :], lall[:, l, :], ACT.Exp, bias=lst[:, l, 1:2], accum_out=lst[:, l, 2:3])
                fn(lcol[:, l, :], lcol[:, l, :], ACT.Exp, bias=lst[:, l, 1:2]).then_inc(setup_act, 1)

            def body(B):
                s, layer = S[B.layer], B.layer

                full, taken = s["work_full"], s["work_taken"]

                def filled(name):
                    act.wait_ge(full, B.use(name) + 1)

                def other(slot):
                    u = slot // 16
                    mo, mu_ = (u + 1) // NG, (u + 1) % NG
                    if B.out(f"MT{u}", slot):
                        filled(f"MT{u}")
                        wait(act, s["mrow_loaded"], B.count(NG * 32, 32 * mu_, mo))
                        fn(mT[:], work[0:2 * G * NT, 0:P // 2].bitcast(BF16), ACT.Copy).then_inc(taken, 1)
                    if B.out("XT", slot):
                        filled("XT")
                        fn(xnT[:, B.parity(2), 1:T + 1], work[:], ACT.Copy).then_inc(taken, 1)
                    for side, name in enumerate(("QT", "KT")):
                        if B.out(name, slot):
                            first_part(side)
                        if B.out(name, slot, 2):
                            second_part(side)
                    if layer == 0:
                        if B.out("FR", slot):
                            filled("FR")
                            fn(fc[:], work[:], ACT.Tanh, scale=0.5).then_inc(taken, 1)
                        if B.out("FK", slot):
                            filled("FK")
                            fn(fd[:], work[:], ACT.Relu).then_inc(taken, 1)
                        for t in range(NT):
                            if B.out(f"PJ{t}", slot):
                                filled(f"PJ{t}")
                                if t == 0:
                                    wait(act, s["vals_done"], B.count(1, 0, 2))
                                fn(big[:, t, :], work[:], ACT.Copy).then_inc(taken, 1)
                        if B.due("VALUES", slot):
                            wait(act, s["pv_done"], B.count(NG * NT, 0))
                            fn(vals[:, B.parity(1), :, :, 0:HD],
                               big[:, :, 3 * P:4 * P].rearrange("p t (h d) -> p t h d", h=H), ACT.Copy
                               ).then_inc(s["vals_done"], 1)
                        if B.out("FT", slot):
                            filled("FT")
                            if B.has(-1):
                                act.wait_ge(s["post"], B.count(2, 2, -1))
                            fn(ffn[:, B.parity(1)].rearrange("p t d -> p (t d)"), work[:], ACT.Copy, scale=0.5
                               ).then_inc(taken, 1)
                        if B.due("SQUARE", slot):
                            act.wait_ge(taken, B.use("PJ3") + 1)
                            fn(sqr[:], big[:, :, 0:2 * P], ACT.Square).then_inc(s["sq_done"], 1)
                        if B.due("ROOT", slot):
                            act.wait_ge(s["rms"], B.count(4, 3, 2))
                            fn(rrms[:], ssq[:], ACT.Sqrt).then_inc(s["root_done"], 1)
                    else:
                        for f in range(NF):
                            if B.out(f"H{f}", slot):
                                filled(f"H{f}")
                                wait(act, s["hidden_done"], B.count(NF, f, 1))
                                fn(fd[:], work[:], ACT.Copy)
                                fn(fa[:], work[:], ACT.Square, scale=GELU_K ** 0.5).then_inc(taken, 1)
                            if B.out(f"H{f}", slot, 2):
                                act.wait_ge(s["gelu"], B.count(NF, f + 1, 1))
                                fn(fc[:], fb[:], ACT.Tanh, scale=GELU_C).then_inc(s["tanh_done"], 1)
                        if B.out("AT", slot):
                            filled("AT")
                            fn(attT[:], work[:], ACT.Copy).then_inc(taken, 1)
                        if B.out("VP", slot):
                            filled("VP")
                            wait(act, s["pv_done"], B.count(NG * NT, 0))
                            fn(vals[:, B.parity(1), :, :, 0:HD].rearrange("p t h d -> p (t h) d"),
                               work[:].rearrange("p (x d) -> p x d", d=HD), ACT.Copy).then_inc(taken, 1)
                        if B.out("Y", slot):
                            filled("Y")
                            if B.has(-1):
                                act.wait_ge(s["post"], B.count(2, 2, -1))
                            fn(ffn[:, B.parity(1)].rearrange("p t d -> p (t d)"), work[:], ACT.Copy
                               ).then_inc(taken, 1)

                def first_part(side):
                    filled(("QT", "KT")[side])
                    wait(act, s["parts_stored"], B.count(32, 0, 2))
                    fn(parts[:, side, 0, :], work[:], ACT.Copy).then_inc(s["part0_done"], 1)

                def second_part(side):
                    act.wait_ge(taken, B.use(("QT", "KT")[side]) + 1)
                    fn(parts[:, side, 1, :], rest[:, side], ACT.Copy).then_inc(s["part1_done"], 1)

                for u in range(NG):
                    for kt in range(NT):
                        for j in range(G):
                            number, pack, tile = TILES[layer][4 * kt + j]
                            if B.has(0) and tile == pack[-1]:
                                if layer == 0 and number == 0:
                                    wait(act, s["pv_done"], B.count(NG * NT, NT * (u - 1)))
                                if layer == 1 and j == 0:
                                    wait(act, s["pv_done"], B.count(NG * NT, NT * (u - 1) + kt + 1))
                                act.wait_ge(s["st_ready"], B.count(NG * EXPS[layer], EXPS[layer] * u + number + 1))
                                row = place(layer, *tile)[0] + (PACK_ROWS * (u % 2) if layer == 0 else 0)
                                fn(probs[:, row, :], st[:, number % 2, :], ACT.Exp, scale=SCALE
                                   ).then_inc(s["exp_done"], 1)
                            eo, eu = (-1, NG - 1) if u == 0 else (0, u - 1)
                            if j == 1 and kt == NT - 1 and B.has(eo):
                                act.wait_ge(s["pv_done"], B.count(NG * NT, NT * eu + NT, eo))
                                if B.has(-1 if u < 2 else 0):
                                    filled(f"OT{u}")
                                fn(accS[:], acc[:], ACT.Copy).then_inc(s["acc_taken"], 1)
                            other(16 * u + 4 * kt + j)
                            yield

            run(body(Body(0, FIRST)))
            border(act, 1)
            run_first_layer(act, body)
            act.wait_ge(S[0]["parts_stored"], 32 * NB)
            run_both_layers(body, 0)
            act.wait_ge(S[0]["mrow_loaded"], NG * 32 * NB)
            run_both_layers(body, 1)
            border(act, 2)
            run_second_layer(act, body)
            border(act, 3)

        @block.vector
        def _(dve):
            v = nc.vector
            dve.wait_ge(setup_in, 16 * SETUP_LOADS)
            v.tensor_copy(causalb[:], causal[:])
            v.tensor_copy(identb[:], ident[:]).then_inc(setup_dve, 1)
            for n in range(6):
                rows = P if n in (2, 3) else 64
                last = v.tensor_copy(rep[0:rows, n], small[0:rows, n, :].unsqueeze(1).broadcast_to([rows, H, HD]))
            last.then_inc(setup_dve, 1)
            dve.wait_ge(setup_pe, 1)
            v.tensor_copy(rep[:, 6], work[:, 0:HD].unsqueeze(1).broadcast_to([P, H, HD])).then_inc(setup_dve, 1)
            for l in range(2):
                last = v.reduce_max(lst[:, l, 0:1], lall[:, l, :], AX_X)
            last.then_inc(rep_chain, 1)
            dve.wait_ge(rep_chain, 1)
            for l in range(2):
                last = v.tensor_scalar(lst[:, l, 1:2], lst[:, l, 0:1], -1.0, None, ALU.mult)
            last.then_inc(setup_dve, 1)
            dve.wait_ge(setup_act, 2)
            for l in range(2):
                last = v.reciprocal(lst[:, l, 3:4], lst[:, l, 2:3])
            last.then_inc(rep_chain, 1)
            dve.wait_ge(rep_chain, 2)
            for l in range(2):
                last = v.tensor_scalar(lcol[:, l, :], lcol[:, l, :], lst[:, l, 3:4], None, ALU.mult)
            last.then_inc(rep_chain, 1)
            dve.wait_ge(rep_chain, 3)
            dve.wait_ge(setup_pe, 2)
            v.tensor_tensor(wcat[:], s1[:, 0, :].rearrange("p (a n) -> p a n", a=4),
                            blocks[:].unsqueeze(1).broadcast_to([P, 4, P]), ALU.mult)
            v.tensor_tensor(normw[:, 1, :], normw[:, 0, :], normw[:, 1, :], ALU.mult).then_inc(rep_chain, 1)
            dve.wait_ge(rep_chain, 4)
            other_map = wcat[:, 2, :].rearrange("p (h d) -> p h d", h=H)
            v.tensor_tensor(other_map, other_map, normw[:, 0, :].unsqueeze(1).broadcast_to([P, H, HD]), ALU.mult)
            v.memset(xnT[:, :, 0:1], 0.0).then_inc(setup_dve, 1)

            def weigh(l):
                dve.wait_ge(compose_in[3 * l], 16)
                rows = (stage_a1, stage_b2)[l].rearrange("p (c n) -> p c n", c=NC)
                v.tensor_tensor(rows, rows, lcol[:, l, :].unsqueeze(2).broadcast_to([P, NC, P]),
                                ALU.mult).then_inc(setup_dve, 1)

            def rest_of_setup():
                weigh(1)
                dve.wait_ge(setup_pe, 3)
                v.memset(vals[:, 0], 0.0).then_inc(rep_chain, 1)
                dve.wait_ge(rep_chain, 5)
                v.memset(vals[:, 0, :, :, HD:HD + 1].rearrange("p t h d -> p (t h) d"), 1.0)
                dve.wait_ge(later_in, 16 * LATER_LOADS)
                v.tensor_scalar(mu[:, 2:4], mu[:, 0:2], -1.0, 1.0, ALU.mult, ALU.add)
                v.tensor_copy(w1[:], st[:, 0, :])
                dve.wait_ge(setup_pe, 4)
                v.tensor_scalar(w2[:].rearrange("p f d -> p (f d)"), st[:, 1, :], 0.5, None, ALU.mult)
                v.memset(stacks[:, 0, 0, :].bitcast(mybir.dt.uint32), 0)

            def body(B):
                s, layer = S[B.layer], B.layer

                full, taken = s["work_full"], s["work_taken"]

                def filled(name):
                    dve.wait_ge(full, B.use(name) + 1)

                def taken_out(name):
                    dve.wait_ge(taken, B.use(name) + 1)

                def link(op, name, per, n, off):
                    op.then_inc(s[name], 1)
                    dve.wait_ge(s[name], B.count(per, n, off))

                def first(u, kt):
                    mo, mu_ = (u + 1) // NG, (u + 1) % NG
                    if kt == 0 and B.has(mo):
                        m = maxs[:, mu_ % 2, :]
                        dve.wait_ge(s["red_done"], B.count(64, 16 * mu_ + 16, mo))
                        link(v.tensor_scalar(msp[:, 0, :], m, -1.0, None, ALU.mult),
                             "msplit", 2 * NG, 2 * mu_ + 1, mo)
                        v.scalar_tensor_tensor(out=msp[:, 1, :], in0=m, scalar=-1.0, in1=msp[:, 0, :],
                                               op0=ALU.mult, op1=ALU.subtract).then_inc(s["msplit"], 1)

                def other(slot):
                    u = slot // 16
                    oo, ou = (-1, u + 2) if u < 2 else (0, u - 2)
                    if B.out(f"OT{u}", slot):
                        filled(f"OT{u}")
                        heads = work[:].rearrange("p (t j c) -> p t j c", t=NT, j=G)
                        link(v.reciprocal(rsum[:], heads[:, :, :, HD]), "rec", NG, ou + 1, oo)
                        if ou == 0 and layer == 0 and B.has(oo - 1):
                            dve.wait_ge(s["post"], B.count(2, 2, oo - 1))
                        v.tensor_tensor(
                            att[:, :, G * HD * ou:G * HD * (ou + 1)].rearrange("p t (j d) -> p t j d", j=G),
                            heads[:, :, :, 0:HD], rsum[:].unsqueeze(3).broadcast_to([P, NT, G, HD]),
                            ALU.mult).then_inc(taken, 1)
                    if B.due("LN", slot):
                        dve.wait_ge(s["x_loaded"], B.count(16, 16, 2))
                        for t in range(NT):
                            last = v.bn_stats(stats[:, t, :], x_tile[:, t, :])
                        last.then_inc(s["ln"], 1)
                        wait_apart(dve, s["ln"], B.count(3, 1, 2), passed)
                        for t in range(NT):
                            last = v.bn_aggr(mv[:, t, :], stats[:, t, :])
                        link(last, "ln", 3, 2, 2)
                        v.tensor_scalar(mv[:, :, 1], mv[:, :, 1], LN_EPS, None, ALU.add).then_inc(s["ln"], 1)
                    if B.due("NORM", slot):
                        dve.wait_ge(s["pow_ln"], B.count(1, 1, 2))
                        for t in range(NT):
                            v.tensor_scalar(xn[:, t, :], x_tile[:, t, :], mv[:, t, 0:1], rstd[:, t:t + 1],
                                            ALU.subtract, ALU.mult).then_inc(s["xn_done"], 1)
                    for side, name in enumerate(("QT", "KT")):
                        if B.out(name, slot, 1):
                            leave_rest(side)
                        if layer == 1 and B.out(name, slot, 3):
                            third_part(side)
                    if layer == 0:
                        if B.due("MIX", slot):
                            xt = xnT[:, B.parity(1), :]
                            for n, mix in enumerate((fa, fb)):
                                link(v.tensor_scalar(mix[:], xt[:, 1:T + 1], mu[:, n:n + 1], None, ALU.mult),
                                     "mix_done", 4, 2 * n + 1, 1)
                                v.scalar_tensor_tensor(out=mix[:], in0=xt[:, 0:T], scalar=mu[:, 2 + n:3 + n],
                                                       in1=mix[:], op0=ALU.mult, op1=ALU.add
                                                       ).then_inc(s["mix_done"], 1)
                        if B.out("FV", slot):
                            filled("FV")
                            v.scalar_tensor_tensor(out=fa[:], in0=fc[:], scalar=1.0, in1=work[:],
                                                   op0=ALU.add, op1=ALU.mult).then_inc(taken, 1)
                        if B.due("MEAN", slot):
                            dve.wait_ge(s["sq_done"], B.count(1, 1, 2))
                            link(v.reduce_sum(ssq[:].rearrange("p (t x) -> p t x", t=NT),
                                              sqr[:].rearrange("p t (x d) -> p t x d", d=HD), AX_X),
                                 "rms", 4, 1, 2)
                            link(v.tensor_scalar(ssq[:], ssq[:], 1.0 / HD, RMS_EPS, ALU.mult, ALU.add),
                                 "rms", 4, 2, 2)
                            v.reciprocal(ssq[:], ssq[:]).then_inc(s["rms"], 1)
                        if B.due("SCALE_QK", slot):
                            dve.wait_ge(s["root_done"], B.count(1, 1, 2))
                            qk = big[:, :, 0:2 * P].rearrange("p t (x d) -> p t x d", d=HD)
                            v.tensor_tensor(qk, qk, rrms[:].rearrange("p (t x) -> p t x", t=NT)
                                            .unsqueeze(3).broadcast_to([P, NT, 2 * H, HD]), ALU.mult
                                            ).then_inc(s["rms"], 1)
                    else:
                        for f in range(NF):
                            if B.out(f"H{f}", slot, 1):
                                gelu_inner(f)
                            if B.out(f"H{f}", slot, 3):
                                gelu_outer(f)
                        if B.out("PR", slot):
                            filled("PR")
                            dve.wait_ge(s["res_loaded"], B.count(16, 16, -1))
                            wait(dve, s["x_stored"], B.count(16, 0, -1))
                            v.tensor_tensor(x_new[:].rearrange("p t d -> p (t d)"), work[:],
                                            x_res[:].rearrange("p t d -> p (t d)"), ALU.add).then_inc(taken, 1)
                            taken_out("PR")
                            link(v.tensor_tensor(x_new[:], x_new[:], ffn[:, B.parity(-1)], ALU.add),
                                 "post", 2, 1, -1)
                            v.tensor_tensor(x_new[:], x_new[:], bproj[:].unsqueeze(1).broadcast_to([P, NT, D]),
                                            ALU.add).then_inc(s["post"], 1)

                def leave_rest(side):
                    filled(("QT", "KT")[side])
                    dve.wait_ge(s["part0_done"], B.count(2, side + 1, 2))
                    v.tensor_tensor(rest[:, side], work[:], parts[:, side, 0, :], ALU.subtract).then_inc(taken, 1)

                def third_part(side):
                    dve.wait_ge(s["part1_done"], B.count(2, side + 1, 2))
                    v.tensor_tensor(parts[:, side, 2, :], rest[:, side], parts[:, side, 1, :],
                                    ALU.subtract).then_inc(s["part2_done"], 1)

                def gelu_inner(f):
                    taken_out(f"H{f}")
                    v.scalar_tensor_tensor(out=fb[:], in0=fa[:], scalar=1.0, in1=fd[:], op0=ALU.add,
                                           op1=ALU.mult).then_inc(s["gelu"], 1)

                def gelu_outer(f):
                    dve.wait_ge(s["tanh_done"], B.count(NF, f + 1, 1))
                    v.scalar_tensor_tensor(out=big[:, f, :], in0=fc[:], scalar=1.0, in1=fd[:],
                                           op0=ALU.add, op1=ALU.mult).then_inc(s["hidden_done"], 1)

                for u in range(NG):
                    for kt in range(NT):
                        first(u, kt)
                        so, su = (0, u + 2) if u < 2 else (1, u - 2)
                        for j in range(NT):
                            m = NT * kt + j
                            if B.has(so) and layer == 0:
                                dve.wait_ge(s["s1_ready"], B.count(64, 16 * su + m + 1, so))
                                v.reduce_max(maxs[:, su % 2, m:m + 1], s1[:, j, 0:P * (j + 1)], AX_X
                                             ).then_inc(s["red_done"], 1)
                            if B.has(so) and layer == 1 and j % 2 == 1:
                                dve.wait_ge(s["s1_ready"], B.count(64, 16 * su + m + 1, so))
                                v.reduce_max(maxs[:, su % 2, m - 1:m + 1], s1[:, j - 1:j + 1, :], AX_X
                                             ).then_inc(s["red_done"], 2)
                            pvo, pu = (-1, NG - 1) if u == 0 else (0, u - 1)
                            if layer == 1 and kt == 1 and j >= POOL_HEADS[pu] and B.has(pvo):
                                dve.wait_ge(s["exp_done"], B.count(64, 16 * pu + 16, pvo))
                                tile = probs[:, G * (NT - 1) + j, :]
                                last = v.tensor_tensor(tile, tile, ebias[:, (NT - 1), :], ALU.mult)
                                if j == G - 1:
                                    last.then_inc(s["emul_dve"], 1)
                            other(16 * u + 4 * kt + j)
                            yield

            weigh(0)
            run(body(Body(0, FIRST)))
            rest_of_setup()
            border(dve, 1)
            run_first_layer(dve, body)
            dve.wait_ge(S[0]["part2_done"], 2 * NB)
            run_both_layers(body, 0)
            dve.wait_ge(S[0]["work_taken"], Body(0, LAST).use("OT0"))
            run_both_layers(body, 1)
            border(dve, 2)
            run_second_layer(dve, body)
            border(dve, 3)

        @block.gpsimd
        def _(pool):
            g = nc.gpsimd
            g.memset(half[:], -0.5)
            g.memset(stacks[:, 1].rearrange("p s n -> p (s n)").bitcast(F32), 0.0).then_inc(setup_pool, 1)
            pool.wait_ge(setup_pool, 1)
            g.memset(stacks[MROW:KROWS, 1, 1, :], 1.0).then_inc(setup_pool, 1)
            pool.wait_ge(setup_pool, 2)

            def rest_of_setup():
                pool.wait_ge(setup_pe, 4)
                g.memset(stacks[:, 0, 1, :].bitcast(F32), 0.0).then_inc(setup_pool, 1)
                pool.wait_ge(setup_pool, 3)
                g.memset(vals[:, 1], 0.0).then_inc(setup_pool, 1)
                pool.wait_ge(setup_pool, 4)
                g.memset(vals[:, 1, :, :, HD:HD + 1].rearrange("p t h d -> p (t h) d"), 1.0)

            def body(B):
                s, layer = S[B.layer], B.layer

                def third_part(side):
                    pool.wait_ge(s["part1_done"], B.count(2, side + 1, 2))
                    g.tensor_tensor(parts[:, side, 2, :], rest[:, side], parts[:, side, 1, :],
                                    ALU.subtract).then_inc(s["part2_done"], 1)

                def other(slot):
                    if B.after("LN", slot, 1):
                        pool.wait_ge(s["ln"], B.count(3, 3, 2))
                        g.tensor_tensor(rstd[:], mv[:, :, 1], half[:, 0:NT], ALU.pow).then_inc(s["pow_ln"], 1)
                    if layer == 0:
                        if B.out("FK", slot, 1):
                            pool.wait_ge(s["work_taken"], B.use("FK") + 1)
                            g.tensor_tensor(fd[:], fd[:], fd[:], ALU.mult).then_inc(s["kact_done"], 1)
                        if B.due("POST", slot):
                            pool.wait_ge(s["work_taken"], B.use("OT1") + 1)
                            pool.wait_ge(s["res_loaded"], B.count(16, 16, -1))
                            wait(pool, s["x_stored"], B.count(16, 0, -1))
                            g.tensor_tensor(x_new[:], x_res[:], att[:], ALU.add).then_inc(s["post"], 1)
                            pool.wait_ge(s["post"], B.count(2, 1, -1))
                            g.tensor_tensor(x_new[:], x_new[:], ffn[:, B.parity(-1)], ALU.add
                                            ).then_inc(s["post"], 1)
                        if B.after("SCALE_QK", slot, 1):
                            pool.wait_ge(s["rms"], B.count(4, 4, 2))
                            k = big[:, :, P:2 * P]
                            kh = k.rearrange("p t (h d) -> p t h d", h=H)
                            g.tensor_tensor(kh, kh, normw[:, 1, :].unsqueeze(1).unsqueeze(1)
                                            .broadcast_to([P, NT, H, HD]), ALU.mult).then_inc(s["k_done"], 1)
                            pool.wait_ge(s["k_done"], B.count(2, 1, 2))
                            g.tensor_tensor(k, k, big[:, :, 2 * P:3 * P], ALU.add).then_inc(s["k_done"], 1)
                        for side, name in enumerate(("QT", "KT")):
                            if B.out(name, slot, 3):
                                third_part(side)

                def mask(off, u, kt):
                    exps = max(n for n, pack in enumerate(PACKS[0]) if (kt, G - 1) in pack) + 1
                    wait_apart(pool, s["exp_done"], B.count(NG * EXPS[0], EXPS[0] * u + exps, off), passed)
                    row, column, width = place(0, kt, 0)
                    row += PACK_ROWS * (u % 2)
                    if kt == 2:
                        diag = probs[:, row:row + G // 2, :].rearrange("p a (b n) -> p (a b) n", n=width)[:, :, 0:P]
                    else:
                        diag = probs[:, row:row + G, column:column + P]
                    g.affine_select(out=diag, in_=diag, compare_op=ALU.is_ge, fill=0.0, base=0,
                                    pattern=[[0, G], [1, P]], channel_multiplier=-1).then_inc(s["masked"], 1)

                for u in range(NG):
                    for kt in range(NT):
                        if layer == 0:
                            mo, mu_ = (-1, NG - 1) if u == 0 else (0, u - 1)
                            if kt < NT - 1 and B.has(mo):
                                mask(mo, mu_, kt + 1)
                            if kt == NT - 1 and B.has(0):
                                mask(0, u, 0)
                        if B.has(0) and layer == 1:
                            n = G if kt < NT - 1 else POOL_HEADS[u]
                            pool.wait_ge(s["exp_done"], B.count(64, 16 * u + 4 * kt + 4))
                            tiles = probs[:, G * kt:G * kt + n, :]
                            g.tensor_tensor(tiles, tiles, ebias[:, kt, :].unsqueeze(1).broadcast_to([P, n, T]),
                                            ALU.mult).then_inc(s["emul_pool"], 1)
                        for j in range(G):
                            other(16 * u + 4 * kt + j)
                            yield

            run(body(Body(0, FIRST)))
            rest_of_setup()
            border(pool, 1)
            run_first_layer(pool, body)
            run_both_layers(body, 0)
            run_both_layers(body, 1)
            border(pool, 2)
            run_second_layer(pool, body)
            border(pool, 3)


def kernel(**inputs):
    import numpy as _np
    import concourse.bacc as _bacc
    from concourse import mybir as _mybir
    from concourse.bass_utils import run_bass_kernel_spmd as _run

    f = {k: _np.asarray(v) for k, v in inputs.items()}
    send = {k: f[k] for k in ("L0_attn_x", "L0_attn_W_DQ", "L0_attn_W_DKV", "L0_attn_W_UKV", "L0_attn_W_QR",
                              "L0_attn_W_KR", "L0_attn_q_norm_w", "L0_attn_k_norm_w", "L1_attn_w_qkv",
                              "L1_attn_w_proj", "L1_attn_b_proj", "L1_ffn_fc1_logits", "L1_ffn_fc2_logits")}
    send["W_UQ_T"] = f["L0_attn_W_UQ"].T
    send["W_UKV_K_T"] = f["L0_attn_W_UKV"][:HD].T
    send["W_O_T"] = f["L0_attn_W_O"].T
    send["W_r_T"] = f["L0_ffn_W_r"].T
    send["W_k_T"] = f["L0_ffn_W_k"].T
    send["W_v_T"] = f["L0_ffn_W_v"].T
    send["mu_r"] = f["L0_ffn_mu_r"].reshape(P, 1)
    send["mu_k"] = f["L0_ffn_mu_k"].reshape(P, 1)
    send["fc1_A_T"] = f["L1_ffn_fc1_A"].transpose(0, 2, 1).reshape(NC * P, D)
    send["fc1_B"] = f["L1_ffn_fc1_B"].reshape(NC * P, FF)
    send["fc2_A_T"] = f["L1_ffn_fc2_A"].transpose(0, 2, 1).reshape(NC * P, FF)
    send["fc2_B"] = f["L1_ffn_fc2_B"].reshape(NC * P, D)
    n = _np.arange(P)
    send["ident"] = _np.eye(P, dtype=_np.float32)
    send["causal"] = _np.where(n[None, :] > n[:, None], NEG, 0.0).astype(_np.float32)
    send["blocks"] = (n[None, :] // HD == n[:, None] // HD).astype(_np.float32)
    pos = _np.mod(_np.arange(T, dtype=_np.float32) * _np.float32((1.0 + _np.sqrt(5.0)) / 2.0), _np.float32(1.0))
    send["ebias"] = (_np.exp(-_np.abs(pos[:, None] - pos[None, :])) + _np.float32(1e-8)).astype(_np.float32)

    nc = _bacc.Bacc("TRN2", target_bir_lowering=False, num_devices=1)
    arrays, args = {}, {}
    for name, value in send.items():
        value = _np.ascontiguousarray(value)
        arrays[f"in_{name}_dram"] = value
        args[name] = nc.dram_tensor(f"in_{name}_dram", value.shape, _mybir.dt.from_np(value.dtype),
                                    kind="ExternalInput").ap()
    out = nc.dram_tensor("out_0_dram", (NB, T, D), _mybir.dt.float32, kind="ExternalOutput").ap()
    build(nc, args, out)
    r = _run(nc, [arrays], core_ids=[0])
    return r.results[0]["out_0_dram"]
```
